# Optimizing a Trainium2 kernel written in Bass

```python
import numpy as np
import jax
import jax.numpy as jnp

def _softmax(x, axis=-1):
    return jax.nn.softmax(x, axis=axis)

def _gelu(x):
    return jax.nn.gelu(x, approximate=True)

def _silu(x):
    return jax.nn.silu(x)

def _sigmoid(x):
    return jax.nn.sigmoid(x)

def _layernorm(x, axis=-1, eps=1e-05):
    m = jnp.mean(x, axis=axis, keepdims=True)
    v = jnp.var(x, axis=axis, keepdims=True)
    return (x - m) / jnp.sqrt(v + eps)

def _scatter_add(tgt, idx, src, axis=0):
    return tgt.at[idx].add(src)

def _segment_sum(src, seg, n):
    return jax.ops.segment_sum(src, seg, n)
kernel_name = 'mk_macaron_d1_jaxref_r8_473f1d'

def setup_inputs(seed: int=0):
    np.random.seed(seed)
    _w = jnp.asarray

    def _L0_attn_setup():
        import jax, jax.numpy as jnp
        import numpy as np
        B, T, D, H, K, V, F = (4, 512, 128, 8, 128, 128, 512)
        EPS = 1e-05

        def layernorm(x, w, b):
            m = jnp.mean(x, -1, keepdims=True)
            v = jnp.var(x, -1, keepdims=True)
            return (x - m) * jax.lax.rsqrt(v + EPS) * w + b

        def l2norm(x):
            return x * jax.lax.rsqrt(jnp.sum(x * x, -1, keepdims=True) + 1e-06)

        def gdn_recurrence(q, k, v, alpha, beta):
            qT = jnp.moveaxis(q, 1, 0)
            kT = jnp.moveaxis(k, 1, 0)
            vT = jnp.moveaxis(v, 1, 0)
            aT = jnp.moveaxis(alpha, 1, 0)
            bT = jnp.moveaxis(beta, 1, 0)

            def step(S, inp):
                q_t, k_t, v_t, a_t, b_t = inp
                kS = jnp.einsum('bhk,bhkv->bhv', k_t, S)
                bk = (b_t[..., None] * k_t)[..., :, None]
                S = a_t[..., None, None] * (S - bk * kS[..., None, :]) + bk * v_t[..., None, :]
                o = jnp.einsum('bhk,bhkv->bhv', q_t, S)
                return (S, o)
            S0 = jnp.zeros((q.shape[0], H, K, V), q.dtype)
            _, oT = jax.lax.scan(step, S0, (qT, kT, vT, aT, bT))
            return jnp.moveaxis(oT, 0, 1)
        key = jax.random.key(seed)
        ks = jax.random.split(key, 12)
        s = 0.02
        return {'x': jax.random.normal(ks[0], (B, T, D), jnp.float32), 'Wq': jax.random.normal(ks[1], (D, H * K), jnp.float32) * s, 'Wk': jax.random.normal(ks[2], (D, H * K), jnp.float32) * s, 'Wv': jax.random.normal(ks[3], (D, H * V), jnp.float32) * s, 'Wb': jax.random.normal(ks[4], (D, H), jnp.float32) * s, 'Wa': jax.random.normal(ks[5], (D, H), jnp.float32) * s, 'Wo': jax.random.normal(ks[6], (H * V, D), jnp.float32) * s, 'ln1_w': jnp.ones((D,), jnp.float32), 'ln1_b': jnp.zeros((D,), jnp.float32), 'ln2_w': jnp.ones((D,), jnp.float32), 'ln2_b': jnp.zeros((D,), jnp.float32), 'W1': jax.random.normal(ks[7], (D, F), jnp.float32) * s, 'b1': jnp.zeros((F,), jnp.float32), 'W2': jax.random.normal(ks[8], (F, D), jnp.float32) * s, 'b2': jnp.zeros((D,), jnp.float32)}
    _L0_attn_in = _L0_attn_setup()

    def _L0_ffn_setup():
        import jax, jax.numpy as jnp
        import numpy as np
        D_IN, D_HID = (128, 512)

        def _ternary(key, shape):
            return jax.random.randint(key, shape, -1, 2).astype(jnp.float32)

        def _tlin(x, w, s):
            return jnp.einsum('bsi,oi->bso', x, w) * s
        key = jax.random.key(seed)
        ks = jax.random.split(key, 12)
        inv = lambda fan: 1.0 / np.sqrt(fan).astype(np.float32)
        return {'x': jax.random.normal(ks[0], (4, 256, D_IN), dtype=jnp.float32), 'w1_w': _ternary(ks[1], (D_HID, D_IN)), 'w1_s': jax.random.uniform(ks[2], (D_HID,), dtype=jnp.float32) * inv(D_IN), 'w2_w': _ternary(ks[3], (D_HID, D_IN)), 'w2_s': jax.random.uniform(ks[4], (D_HID,), dtype=jnp.float32) * inv(D_IN), 'h1_w': _ternary(ks[5], (D_HID, D_HID)), 'h1_s': jax.random.uniform(ks[6], (D_HID,), dtype=jnp.float32) * inv(D_HID), 'h2_w': _ternary(ks[7], (D_HID, D_HID)), 'h2_s': jax.random.uniform(ks[8], (D_HID,), dtype=jnp.float32) * inv(D_HID), 'w3_w': _ternary(ks[9], (D_IN, D_HID)), 'w3_s': jax.random.uniform(ks[10], (D_IN,), dtype=jnp.float32) * inv(D_HID)}
    _L0_ffn_in = _L0_ffn_setup()
    _d = {'L0_attn_x': _L0_attn_in['x'], 'L0_attn_Wq': _L0_attn_in['Wq'], 'L0_attn_Wk': _L0_attn_in['Wk'], 'L0_attn_Wv': _L0_attn_in['Wv'], 'L0_attn_Wb': _L0_attn_in['Wb'], 'L0_attn_Wa': _L0_attn_in['Wa'], 'L0_attn_Wo': _L0_attn_in['Wo'], 'L0_attn_ln1_w': _L0_attn_in['ln1_w'], 'L0_attn_ln1_b': _L0_attn_in['ln1_b'], 'L0_attn_ln2_w': _L0_attn_in['ln2_w'], 'L0_attn_ln2_b': _L0_attn_in['ln2_b'], 'L0_attn_W1': _L0_attn_in['W1'], 'L0_attn_b1': _L0_attn_in['b1'], 'L0_attn_W2': _L0_attn_in['W2'], 'L0_attn_b2': _L0_attn_in['b2'], 'L0_ffn_w1_w': _L0_ffn_in['w1_w'], 'L0_ffn_w1_s': _L0_ffn_in['w1_s'], 'L0_ffn_w2_w': _L0_ffn_in['w2_w'], 'L0_ffn_w2_s': _L0_ffn_in['w2_s'], 'L0_ffn_h1_w': _L0_ffn_in['h1_w'], 'L0_ffn_h1_s': _L0_ffn_in['h1_s'], 'L0_ffn_h2_w': _L0_ffn_in['h2_w'], 'L0_ffn_h2_s': _L0_ffn_in['h2_s'], 'L0_ffn_w3_w': _L0_ffn_in['w3_w'], 'L0_ffn_w3_s': _L0_ffn_in['w3_s']}
    _x0 = _d['L0_attn_x']
    _d['L0_attn_x'] = jax.random.normal(jax.random.fold_in(jax.random.key(seed), 1), (8, 512, 128), dtype=_x0.dtype)
    del _x0
    return _d

def reference(L0_attn_x, L0_attn_Wq, L0_attn_Wk, L0_attn_Wv, L0_attn_Wb, L0_attn_Wa, L0_attn_Wo, L0_attn_ln1_w, L0_attn_ln1_b, L0_attn_ln2_w, L0_attn_ln2_b, L0_attn_W1, L0_attn_b1, L0_attn_W2, L0_attn_b2, L0_ffn_w1_w, L0_ffn_w1_s, L0_ffn_w2_w, L0_ffn_w2_s, L0_ffn_h1_w, L0_ffn_h1_s, L0_ffn_h2_w, L0_ffn_h2_s, L0_ffn_w3_w, L0_ffn_w3_s):

    def _L0_attn_ref(x, Wq, Wk, Wv, Wb, Wa, Wo, ln1_w, ln1_b, ln2_w, ln2_b, W1, b1, W2, b2):
        import jax, jax.numpy as jnp
        import numpy as np
        B, T, D, H, K, V, F = (4, 512, 128, 8, 128, 128, 512)
        EPS = 1e-05

        def layernorm(x, w, b):
            m = jnp.mean(x, -1, keepdims=True)
            v = jnp.var(x, -1, keepdims=True)
            return (x - m) * jax.lax.rsqrt(v + EPS) * w + b

        def l2norm(x):
            return x * jax.lax.rsqrt(jnp.sum(x * x, -1, keepdims=True) + 1e-06)

        def gdn_recurrence(q, k, v, alpha, beta):
            qT = jnp.moveaxis(q, 1, 0)
            kT = jnp.moveaxis(k, 1, 0)
            vT = jnp.moveaxis(v, 1, 0)
            aT = jnp.moveaxis(alpha, 1, 0)
            bT = jnp.moveaxis(beta, 1, 0)

            def step(S, inp):
                q_t, k_t, v_t, a_t, b_t = inp
                kS = jnp.einsum('bhk,bhkv->bhv', k_t, S)
                bk = (b_t[..., None] * k_t)[..., :, None]
                S = a_t[..., None, None] * (S - bk * kS[..., None, :]) + bk * v_t[..., None, :]
                o = jnp.einsum('bhk,bhkv->bhv', q_t, S)
                return (S, o)
            S0 = jnp.zeros((q.shape[0], H, K, V), q.dtype)
            _, oT = jax.lax.scan(step, S0, (qT, kT, vT, aT, bT))
            return jnp.moveaxis(oT, 0, 1)
        b, t, _ = x.shape
        n = layernorm(x, ln1_w, ln1_b)
        q = l2norm(jax.nn.silu(n @ Wq).reshape(b, t, H, K))
        k = l2norm(jax.nn.silu(n @ Wk).reshape(b, t, H, K))
        v = jax.nn.silu(n @ Wv).reshape(b, t, H, V)
        beta = jax.nn.sigmoid(n @ Wb)
        alpha = jax.nn.sigmoid(n @ Wa)
        o = gdn_recurrence(q, k, v, alpha, beta).reshape(b, t, H * V) @ Wo
        x = x + o
        h = layernorm(x, ln2_w, ln2_b)
        x = x + (jax.nn.gelu(h @ W1 + b1, approximate=False) @ W2 + b2)
        return x

    def _L0_ffn_ref(x, w1_w, w1_s, w2_w, w2_s, h1_w, h1_s, h2_w, h2_s, w3_w, w3_s):
        import jax, jax.numpy as jnp
        import numpy as np
        D_IN, D_HID = (128, 512)

        def _ternary(key, shape):
            return jax.random.randint(key, shape, -1, 2).astype(jnp.float32)

        def _tlin(x, w, s):
            return jnp.einsum('bsi,oi->bso', x, w) * s
        h = jax.nn.silu(_tlin(x, w1_w, w1_s)) * _tlin(x, w2_w, w2_s)
        h = jax.nn.gelu(_tlin(h, h1_w, h1_s), approximate=False)
        h = jax.nn.gelu(_tlin(h, h2_w, h2_s), approximate=False)
        return _tlin(h, w3_w, w3_s)
    x = L0_attn_x
    x = x + 0.5 * _L0_ffn_ref(_layernorm(x, axis=-1), L0_ffn_w1_w, L0_ffn_w1_s, L0_ffn_w2_w, L0_ffn_w2_s, L0_ffn_h1_w, L0_ffn_h1_s, L0_ffn_h2_w, L0_ffn_h2_s, L0_ffn_w3_w, L0_ffn_w3_s)
    x = x + _L0_attn_ref(_layernorm(x, axis=-1), L0_attn_Wq, L0_attn_Wk, L0_attn_Wv, L0_attn_Wb, L0_attn_Wa, L0_attn_Wo, L0_attn_ln1_w, L0_attn_ln1_b, L0_attn_ln2_w, L0_attn_ln2_b, L0_attn_W1, L0_attn_b1, L0_attn_W2, L0_attn_b2)
    x = x + 0.5 * _L0_ffn_ref(_layernorm(x, axis=-1), L0_ffn_w1_w, L0_ffn_w1_s, L0_ffn_w2_w, L0_ffn_w2_s, L0_ffn_h1_w, L0_ffn_h1_s, L0_ffn_h2_w, L0_ffn_h2_s, L0_ffn_w3_w, L0_ffn_w3_s)
    return x

_drawn_inputs = setup_inputs


def setup_inputs(seed=0):
    import zlib

    import numpy as np

    out = dict(_drawn_inputs(seed))
    spreads = {'L0_attn_ln1_w': (1.0, 0.2),
     'L0_attn_ln1_b': (0.0, 0.1),
     'L0_attn_ln2_w': (1.0, 0.2),
     'L0_attn_ln2_b': (0.0, 0.1),
     'L0_attn_b1': (0.0, 0.1),
     'L0_attn_b2': (0.0, 0.1)}
    factors = {}
    for name, (base, spread) in spreads.items():
        noise = np.random.default_rng([zlib.crc32(name.encode()), seed]).standard_normal(out[name].shape)
        drawn = base * np.exp(spread * noise) if base else spread * noise
        out[name] = jnp.asarray(drawn.astype(out[name].dtype))
    for name, factor in factors.items():
        out[name] = (out[name] * factor).astype(out[name].dtype)
    return out
```

```python
from contextlib import ExitStack

import concourse.bass as bass
from concourse import mybir

B, T, D, H, HID = 8, 512, 128, 8, 512
C = 128
NC = T // C
U = NC * H
KB = HID // 128
BS = 32
NBLK = C // BS
EPS_LN, EPS_L2 = 1e-5, 1e-6
NEG = -1e30
RSQRT_STEPS = 11


def build_program(nc, d):
    f32, f32r, bf16, i32 = mybir.dt.float32, mybir.dt.float32r, mybir.dt.bfloat16, mybir.dt.int32
    ALU, ACT, AX = mybir.AluOpType, mybir.ActivationFunctionType, mybir.AxisListType
    ctx = ExitStack()
    with ctx:
        def sb(name, shape, dt=f32):
            return ctx.enter_context(nc.sbuf_tensor(name, shape, dt))

        def sem(name):
            return ctx.enter_context(nc.semaphore(name))

        w1 = sb("w1", [128, HID])
        w2 = sb("w2", [128, HID])
        h1 = sb("h1", [128, KB, HID])
        h2 = sb("h2", [128, KB, HID])
        w3 = sb("w3", [128, KB, D])
        wqkv = sb("wqkv", [128, 3, H * 128])
        wba = sb("wba", [128, 2 * H])
        wo = sb("wo", [128, H, D])
        wm1 = sb("wm1", [128, HID])
        wm2 = sb("wm2", [128, KB, D])
        cols = sb("cols", [128, 24])
        s1, s2, sh1, sh2, b1 = (cols[:, 4 * i:4 * i + 4] for i in range(5))
        ln1w, ln1b, ln2w, ln2b = (cols[:, 20 + i:21 + i] for i in range(4))
        s3row = sb("s3row", [128, D])
        b2row = sb("b2row", [128, D])

        ident = sb("ident", [128, 128])
        identb = sb("identb", [128, 128], bf16)
        triu = sb("triu", [128, 128])
        triur = sb("triur", [128, 128], f32r)
        ones = sb("ones", [128, 1])
        maskb = sb("maskb", [128, 128], bf16)

        xin = sb("xin", [128, NC, D])
        x1 = sb("x1", [128, NC, D])
        x1m = sb("x1m", [128, NC, D])
        x2 = sb("x2", [128, NC, D])
        n0 = sb("n0", [128, NC, D])
        xa = sb("xa", [128, NC, D])
        xn1 = sb("xn1", [128, NC, D])
        rows_and_qe = sb("rows_and_qe", [128, 2 * T])
        xn = rows_and_qe[:, 0:T].rearrange("p (c n) -> p c n", c=NC)
        xT = rows_and_qe[:, T:2 * T]
        qe = rows_and_qe[:, :].rearrange("p (h n) -> p h n", h=H)
        nT = sb("nT", [128, T])

        big = [sb("big0", [128, 2 * H * 128]), sb("big1", [128, 2 * H * 128])]
        hid = [t[:, :].rearrange("p (k n) -> p k n", k=KB) for t in big]
        qk = [t[:, :].rearrange("p (s h n) -> p s h n", s=2, h=H) for t in big]
        pneg32 = big[0][:, 0:U * BS].rearrange("p (u n) -> p u n", u=U)
        pneg64 = big[1][:, 0:U * 64].rearrange("p (u n) -> p u n", u=U)
        mid = sb("mid", [128, H * 128])
        sg = mid[:, :].rearrange("p (s n) -> p s n", s=2)
        qT = mid[:, :].rearrange("p (h n) -> p h n", h=H)
        oT = qT

        V = sb("V", [128, U, 128])
        KD = sb("KD", [128, U, 128])
        KT = sb("KT", [128, U, 128])
        QET = sb("QET", [128, U, 128])
        R = sb("R", [128, U, 128])
        MT = sb("MT", [128, U, 128])
        TB = sb("TB", [128, U, 64])
        state = sb("state", [128, H, 128])
        blkA = sb("blkA", [128, BS * BS])
        blkT = sb("blkT", [128, BS * BS])
        blkP = sb("blkP", [128, 256])

        absz = sb("absz", [128, NC * 2 * H])
        ez = sb("ez", [128, NC * 2 * H])
        lz = sb("lz", [128, NC * 2 * H])
        lgb = sb("lgb", [128, U])
        lga = sb("lga", [128, U])
        lah = sb("lah", [128, U], f32r)
        lal = sb("lal", [128, U], f32r)
        biasj = sb("biasj", [128, U])
        kdl = sb("kdl", [128, U])
        kds = sb("kds", [128, U])
        eg = sb("eg", [128, U])
        egn = sb("egn", [128, U])
        egC = sb("egC", [128, U])
        bst = sb("bst", [128, 2 * H, 6])
        bsq = sb("bsq", [128, 2 * H, 2])
        bss = sb("bss", [128, 2 * H, 2])
        ssq = sb("ssq", [128, 2 * H])
        rnorm = sb("rnorm", [128, 2 * H])
        rtmp = sb("rtmp", [128, 2 * H])
        rtmp2 = sb("rtmp2", [128, 2 * H])

        bank = [ctx.enter_context(nc.psum_tensor(f"bank{i}", [128, 512], f32)) for i in range(8)]

        def heads(bk):
            return bk[:, :].rearrange("p (h n) -> p h n", h=4)

        blocks_out = nc.dram_tensor("blocks_out", [NBLK, U, BS, BS], f32).ap()
        t_back = nc.dram_tensor("t_back", [NBLK, U, BS, BS], f32).ap()
        r_back = nc.dram_tensor("r_back", [NBLK, U, BS, BS], f32).ap()

        ld_x = sem("ld_x")
        ld_w = sem("ld_w")
        ld_a = sem("ld_a")
        c_mem = sem("c_mem")
        c_pool = sem("c_pool")
        c_dve = sem("c_dve")
        st_out = sem("st_out")

        class Site:
            def __init__(self, n):
                self.stats, self.aggr, self.var = sem(n + "_stats"), sem(n + "_aggr"), sem(n + "_var")
                self.sq, self.newton, self.rows = sem(n + "_sq"), sem(n + "_newton"), sem(n + "_rows")
                self.st, self.mean = sb(n + "_st", [128, NC, 6]), sb(n + "_mean", [128, NC])
                self.ve, self.rs = sb(n + "_ve", [128, NC]), sb(n + "_rs", [128, NC])
                self.ta, self.tb = sb(n + "_ta", [128, NC]), sb(n + "_tb", [128, NC])

        ln_f = {"f1": Site("lnf1"), "f2": Site("lnf2")}
        ln_m, ln_n0, ln_n1 = Site("lnm"), Site("lnn0"), Site("lnn1")

        def ffn_sems(n):
            names = ("tr", "xT", "gate", "silu", "hid", "l2", "g2", "l3", "g3", "l4", "sc", "res")
            return {k: sem(f"{n}_{k}") for k in names}

        F = {"f1": ffn_sems("f1"), "f2": ffn_sems("f2")}
        x1_moved = sem("x1_moved")
        n_tr, n_nT, n_logit = sem("n_tr"), sem("n_nT"), sem("n_logit")
        n_abs, n_exp, n_ln, n_lg, n_hi, n_lo = (sem("n_" + k) for k in ("abs", "exp", "ln", "lg", "hi", "lo"))
        p_g, p_gexp, p_bias, p_kdl, p_kds, p_egn = (sem("p_" + k) for k in ("g", "gexp", "bias", "kdl", "kds", "egn"))
        p_d, p_dexp = sem("p_d"), sem("p_dexp")
        p_proj, p_silu = sem("p_proj"), sem("p_silu")
        p_bst, p_ss1, p_ss2, p_ssq = (sem("p_" + k) for k in ("bst", "ss1", "ss2", "ssq"))
        p_newton = sem("p_newton")
        p_unit, p_kd, p_qe = sem("p_unit"), sem("p_kd"), sem("p_qe")
        p_tr, p_trc = sem("p_tr"), sem("p_trc")
        p_kq, p_am = sem("p_kq"), sem("p_am")
        b_out, b_in = sem("b_out"), sem("b_in")
        b_init, b_prod, b_R = sem("b_init"), sem("b_prod"), sem("b_R")
        b_back, b_load = sem("b_back"), sem("b_load")
        j_p32, j_p32c0, j_p32c1 = sem("j_p32"), sem("j_p32c0"), sem("j_p32c1")
        j_t, j_tc, j_r01, j_r01c, j_r23, j_r23c = (sem("j_" + k) for k in ("t", "tc", "r01", "r01c", "r23", "r23c"))
        j_p64, j_p64v, j_p64a = sem("j_p64"), sem("j_p64v"), sem("j_p64a")
        j_r, j_rv, j_ra = sem("j_r"), sem("j_rv"), sem("j_ra")
        s_ks, s_rhs = sem("s_ks"), sem("s_rhs")
        s_w, s_wc = sem("s_w"), sem("s_wc")
        s_up, s_S = sem("s_up"), sem("s_S")
        s_o, s_oc = sem("s_o"), sem("s_oc")
        s_y, s_xa = sem("s_y"), sem("s_xa")
        m_tr, m_xT, m_up, m_gelu, m_down = (sem("m_" + k) for k in ("tr", "xT", "up", "gelu", "down"))
        m_xab, m_xab2, m_x2 = sem("m_xab"), sem("m_xab2"), sem("m_x2")

        block = ctx.enter_context(nc.Block())

        @block.sync
        def _(sp):
            def load_x(b):
                sp.dma_start(xin[:, :, :], d["x"][bass.ds(b, 1), :, :].rearrange("o (c p) n -> p (o c) n", p=128)
                             ).then_inc(ld_x, 16)

            load_x(0)
            for dst, src in ((w1[:, :], d["w1T"]), (w2[:, :], d["w2T"]), (cols[:, :], d["cols"]),
                             (h1[:, :, :], d["h1T"].rearrange("(k p) n -> p k n", p=128)),
                             (h2[:, :, :], d["h2T"].rearrange("(k p) n -> p k n", p=128)),
                             (w3[:, :, :], d["w3T"].rearrange("(k p) n -> p k n", p=128)),
                             (s3row[:, :], d["s3"].partition_broadcast(128)),
                             (b2row[:, :], d["b2"].partition_broadcast(128))):
                sp.dma_start(dst, src).then_inc(ld_w, 16)
            for dst, src in ((wba[:, 0:H], d["Wb"]), (wba[:, H:], d["Wa"]),
                             (wqkv[:, 0, :], d["Wq"]), (wqkv[:, 1, :], d["Wk"]), (wqkv[:, 2, :], d["Wv"]),
                             (wo[:, :, :], d["Wo"].rearrange("(h p) n -> p h n", p=128)),
                             (wm1[:, :], d["W1"]),
                             (wm2[:, :, :], d["W2"].rearrange("(k p) n -> p k n", p=128))):
                sp.dma_start(dst, src).then_inc(ld_a, 16)

            def P(b):
                for c in range(NC):
                    sp.wait_ge(p_am, b * 16 + 4 * c + 4)
                    for p in range(NBLK):
                        r = slice(BS * p, BS * p + BS)
                        sp.dma_start(blocks_out[p, H * c:H * c + H, :, :].rearrange("u j i -> j u i"),
                                     R[r, H * c:H * c + H, r]).then_inc(b_out, 16)
                sp.wait_ge(b_out, b * 256 + 256)
                sp.dma_start(blkA[:, :], blocks_out.rearrange("p u j i -> (p u) (j i)")).then_inc(b_in, 16)

            def F1(b):
                sp.wait_ge(F["f1"]["res"], b + 1)

            def F1_next(b):
                F1(b)
                load_x(b + 1)

            def back(b):
                sp.wait_ge(b_prod, b * 2 * (BS - 1) + 2 * (BS - 1))
                sp.dma_start(t_back.rearrange("p u i c -> (p u) (i c)"), blkT[:, :]).then_inc(b_back, 16)
                sp.wait_ge(b_R, b + 1)
                sp.dma_start(r_back.rearrange("p u c i -> (p u) (c i)"), blkA[:, :]).then_inc(b_back, 16)
                sp.wait_ge(b_back, b * 32 + 32)
                for p in range(NBLK):
                    r = slice(BS * p, BS * p + BS)
                    sp.dma_start(R[r, :, r], r_back[p, :, :, :].rearrange("u c i -> c u i")).then_inc(b_load, 16)
                for p, col in ((0, 0), (1, BS), (2, 0)):
                    sp.dma_start(TB[BS * p:BS * p + BS, :, col:col + BS],
                                 t_back[p, :, :, :].rearrange("u i c -> i u c")).then_inc(b_load, 16)

            def F2(b):
                sp.wait_ge(F["f2"]["res"], b + 1)
                sp.dma_start(d["out"][bass.ds(b, 1), :, :].rearrange("o (c p) n -> p (o c) n", p=128),
                             x2[:, :, :]).then_inc(st_out, 16)

            F1_next(0), P(0), back(0), F1_next(1)
            with sp.Fori(1, B - 2) as t:
                P(t), back(t), F1_next(t + 1), F2(t - 1)
            P(B - 2), back(B - 2), F2(B - 3)
            P(B - 1), back(B - 1), F2(B - 2), F2(B - 1)
            sp.wait_ge(st_out, B * 16)

        @block.gpsimd
        def _(pool):
            pool.memset(ident[:, :], 0.0)
            pool.memset(triu[:, :], 1.0)
            pool.memset(identb[:, :], 0.0)
            pool.memset(maskb[:, :], 0.0).then_inc(c_mem, 1)
            pool.memset(ones[:, :], 1.0)
            pool.memset(TB[:, :, :], 0.0)
            pool.wait_ge(c_mem, 1)
            pool.affine_select(out=ident[:, :], in_=ident[:, :], compare_op=ALU.not_equal, fill=1.0,
                               base=0, pattern=[[-1, 128]], channel_multiplier=1)
            pool.affine_select(out=identb[:, :], in_=identb[:, :], compare_op=ALU.not_equal, fill=1.0,
                               base=0, pattern=[[-1, 128]], channel_multiplier=1)
            pool.affine_select(out=triu[:, :], in_=triu[:, :], compare_op=ALU.is_ge, fill=0.0,
                               base=0, pattern=[[1, 128]], channel_multiplier=-1)
            pool.affine_select(out=maskb[:, :], in_=maskb[:, :], compare_op=ALU.is_ge, fill=NEG,
                               base=0, pattern=[[1, 128]], channel_multiplier=-1).then_inc(c_pool, 1)

            def P(b):
                for c in range(NC):
                    u = slice(H * c, H * c + H)
                    pool.wait_ge(p_unit, b * NC + c + 1)
                    if c == 0:
                        pool.wait_ge(p_kds, b + 1)
                        pool.wait_ge(p_gexp, b + 1)
                    pool.tensor_tensor(KD[:, u, :], qk[c % 2][:, 1, :, :],
                                       kds[:, u].unsqueeze(2).to_broadcast([128, H, 128]), ALU.mult).then_inc(p_kd, 1)
                    if c > 0:
                        pool.wait_ge(p_tr, b * 6 * NC + 6 * c)
                    pool.tensor_tensor(qe[:, :, :], qk[c % 2][:, 0, :, :],
                                       eg[:, u].unsqueeze(2).to_broadcast([128, H, 128]), ALU.mult).then_inc(p_qe, 1)

            A3 = blkA[:, :].rearrange("q (j i) -> q j i", j=BS)
            T3 = blkT[:, :].rearrange("q (i c) -> q i c", i=BS)

            def invert(b):
                pool.wait_ge(b_init, b * 2 + 2)
                pool.wait_ge(b_in, b * 16 + 16)
                steps = 2 * (BS - 1)
                for j in range(BS - 1):
                    n, m = BS - 1 - j, j + 1
                    prod = blkP[:, 0:n * m].rearrange("q (i c) -> q i c", i=n)
                    if j > 0:
                        pool.wait_ge(b_prod, b * steps + 2 * j)
                    pool.tensor_tensor(prod, A3[:, j, j + 1:].unsqueeze(2).to_broadcast([128, n, m]),
                                       T3[:, j:j + 1, 0:m].to_broadcast([128, n, m]), ALU.mult).then_inc(b_prod, 1)
                    pool.wait_ge(b_prod, b * steps + 2 * j + 1)
                    pool.tensor_tensor(T3[:, j + 1:, 0:m], T3[:, j + 1:, 0:m], prod, ALU.subtract).then_inc(b_prod, 1)
                pool.wait_ge(b_prod, b * steps + steps)
                pool.tensor_tensor(A3, T3.rearrange("q i c -> q c i"),
                                   ones[:, :].unsqueeze(2).to_broadcast([128, BS, BS]), ALU.mult).then_inc(b_R, 1)

            def M(b):
                pool.wait_ge(s_xa, b * NC + NC)
                pool.wait_ge(x1_moved, b + 1)
                pool.tensor_tensor(x1m[:, :, :], xa[:, :, :], x1m[:, :, :], ALU.add).then_inc(m_xab, 1)
                pool.wait_ge(m_xab, b + 1)
                pool.tensor_tensor(x1m[:, :, :], x1m[:, :, :],
                                   b2row[:, :].unsqueeze(1).to_broadcast([128, NC, D]), ALU.add).then_inc(m_xab2, 1)

            def P_invert(b):
                P(b), invert(b)

            pool.wait_ge(ld_w, 8 * 16)
            P_invert(0)
            with pool.Fori(1, B) as t:
                P(t), M(t - 1), invert(t)
            M(B - 1)

        @block.vector
        def _(dve):
            dve.wait_ge(c_pool, 1)
            dve.tensor_copy(triur[:, :], triu[:, :])
            dve.wait_ge(ld_w, 8 * 16)
            dve.tensor_scalar(s3row[:, :], s3row[:, :], 0.5, None, ALU.mult).then_inc(c_dve, 1)

            def rsqrt(done, b, x, y, ta, tb):
                n = b * RSQRT_STEPS
                dve.tensor_scalar(ta.bitcast(i32), x.bitcast(i32), 1, None, ALU.arith_shift_right).then_inc(done, 1)
                dve.wait_ge(done, n + 1)
                dve.tensor_scalar(y.bitcast(i32), ta.bitcast(i32), -1, 0x5F3759DF, ALU.mult, ALU.add).then_inc(done, 1)
                for i in range(3):
                    dve.wait_ge(done, n + 3 * i + 2)
                    dve.tensor_tensor(ta, y, y, ALU.mult).then_inc(done, 1)
                    dve.wait_ge(done, n + 3 * i + 3)
                    dve.scalar_tensor_tensor(out=tb, in0=ta, scalar=-0.5, in1=x, op0=ALU.mult, op1=ALU.mult
                                             ).then_inc(done, 1)
                    dve.wait_ge(done, n + 3 * i + 4)
                    dve.scalar_tensor_tensor(out=y, in0=tb, scalar=1.5, in1=y, op0=ALU.add, op1=ALU.mult
                                             ).then_inc(done, 1)
                dve.wait_ge(done, n + RSQRT_STEPS)

            def layernorm(s, b, x, out):
                for c in range(NC):
                    last = dve.bn_stats(s.st[:, c, :], x[:, c, :])
                last.then_inc(s.stats, 1)
                dve.wait_ge(s.stats, b + 1)
                dve.tensor_tensor(s.mean[:, :], s.st[:, :, 1], s.st[:, :, 4], ALU.add)
                dve.tensor_tensor(s.ta[:, :], s.st[:, :, 1], s.st[:, :, 4], ALU.subtract)
                dve.tensor_tensor(s.tb[:, :], s.st[:, :, 2], s.st[:, :, 5], ALU.add).then_inc(s.aggr, 1)
                dve.wait_ge(s.aggr, b + 1)
                dve.tensor_scalar(s.mean[:, :], s.mean[:, :], 0.5, None, ALU.mult)
                dve.tensor_scalar(s.ve[:, :], s.tb[:, :], 1.0 / D, EPS_LN, ALU.mult, ALU.add)
                dve.scalar_tensor_tensor(out=s.ta[:, :], in0=s.ta[:, :], scalar=0.25, in1=s.ta[:, :],
                                         op0=ALU.mult, op1=ALU.mult).then_inc(s.sq, 1)
                dve.wait_ge(s.sq, b + 1)
                dve.tensor_tensor(s.ve[:, :], s.ve[:, :], s.ta[:, :], ALU.add).then_inc(s.var, 1)
                dve.wait_ge(s.var, b + 1)
                rsqrt(s.newton, b, s.ve[:, :], s.rs[:, :], s.ta[:, :], s.tb[:, :])
                for c in range(NC):
                    last = dve.tensor_scalar(out[:, c, :], x[:, c, :], s.mean[:, c:c + 1], s.rs[:, c:c + 1],
                                             ALU.subtract, ALU.mult)
                last.then_inc(s.rows, 1)

            def ffn(n, b, x, out):
                f, s = F[n], ln_f[n]
                layernorm(s, b, x, xn)
                for o in range(KB):
                    dve.wait_ge(f["gate"], b * 2 * KB + 2 * o + 2)
                    dve.wait_ge(f["silu"], b * KB + o + 1)
                    dve.scalar_tensor_tensor(out=hid[0][:, o, :], in0=bank[1 + 2 * (o % 2)][:, :], scalar=s2[:, o:o + 1],
                                             in1=sg[:, o % 2, :], op0=ALU.mult, op1=ALU.mult).then_inc(f["hid"], 1)
                for c in range(NC):
                    dve.wait_ge(f["l4"], b * NC + c + 1)
                    last = dve.tensor_tensor(xn[:, c, :], bank[4 + c][:, 0:D], s3row[:, :], ALU.mult)
                last.then_inc(f["sc"], 1)
                dve.wait_ge(f["sc"], b + 1)
                dve.tensor_tensor(out[:, :, :], xn[:, :, :], x[:, :, :], ALU.add).then_inc(f["res"], 1)

            def F1(b):
                dve.wait_ge(ld_x, b * 16 + 16)
                ffn("f1", b, xin, x1)

            def F2(b):
                ffn("f2", b, x2, x2)

            def N(b):
                dve.wait_ge(F["f1"]["res"], b + 1)
                layernorm(ln_n0, b, x1, n0)
                dve.wait_ge(ln_n0.rows, b + 1)
                layernorm(ln_n1, b, n0, xn1)

            def gates(b):
                dve.wait_ge(n_logit, b + 1)
                z = bank[1][:, 0:NC * 2 * H]
                dve.tensor_scalar(lz[:, :], z, -1.0, None, ALU.mult).then_inc(n_abs, 1)
                dve.wait_ge(n_abs, b * 2 + 1)
                dve.tensor_tensor(absz[:, :], z, lz[:, :], ALU.max).then_inc(n_abs, 1)
                dve.wait_ge(n_ln, b + 1)
                z4 = z.rearrange("p (c s h) -> p c s h", c=NC, s=2)
                l4 = lz[:, :].rearrange("p (c s h) -> p c s h", c=NC, s=2)
                for s, dst in ((0, lgb), (1, lga)):
                    last = dve.scalar_tensor_tensor(out=dst[:, :].rearrange("p (c h) -> p c h", c=NC), in0=z4[:, :, s, :],
                                                    scalar=0.0, in1=l4[:, :, s, :], op0=ALU.min, op1=ALU.subtract)
                last.then_inc(n_lg, 1)
                dve.wait_ge(n_lg, b + 1)
                dve.tensor_copy(lah[:, :], lga[:, :]).then_inc(n_hi, 1)
                dve.wait_ge(n_hi, b + 1)
                dve.tensor_tensor(lal[:, :], lga[:, :], lah[:, :].bitcast(f32), ALU.subtract).then_inc(n_lo, 1)

            def P(b):
                if not isinstance(b, int) or b > 0:
                    dve.wait_ge(b_back, b * 32)
                dve.memset(blkT[:, :], 0.0).then_inc(b_init, 1)
                dve.wait_ge(b_init, b * 2 + 1)
                dve.memset(blkT[:, 0:BS * BS:BS + 1], 1.0).then_inc(b_init, 1)
                dve.wait_ge(p_g, b + 1)
                dve.tensor_tensor(biasj[:, :], lgb[:, :], bank[1][:, 0:U], ALU.subtract).then_inc(p_bias, 1)
                dve.wait_ge(p_bias, b + 1)
                dve.tensor_tensor(kdl[:, :], biasj[:, :], bank[1][:, U:2 * U], ALU.add).then_inc(p_kdl, 1)
                dve.wait_ge(p_gexp, b + 1)
                dve.tensor_scalar(egn[:, :], eg[:, :], -1.0, None, ALU.mult).then_inc(p_egn, 1)

                def unit(c):
                    rows = qk[c % 2]
                    dve.wait_ge(p_silu, b * 6 * NC + 6 * c + 4)
                    for i in range(2 * H):
                        last = dve.bn_stats(bst[:, i, :], rows[:, i // H, i % H, :])
                    last.then_inc(p_bst, 1)
                    k = b * NC + c
                    dve.wait_ge(p_bst, k + 1)
                    dve.tensor_tensor(bsq[:, :, :], bst[:, :, 1::3], bst[:, :, 1::3], ALU.mult).then_inc(p_ss1, 1)
                    dve.wait_ge(p_ss1, k + 1)
                    dve.scalar_tensor_tensor(out=bss[:, :, :], in0=bsq[:, :, :], scalar=64.0, in1=bst[:, :, 2::3],
                                             op0=ALU.mult, op1=ALU.add).then_inc(p_ss2, 1)
                    dve.wait_ge(p_ss2, k + 1)
                    dve.scalar_tensor_tensor(out=ssq[:, :], in0=bss[:, :, 0], scalar=EPS_L2, in1=bss[:, :, 1],
                                             op0=ALU.add, op1=ALU.add).then_inc(p_ssq, 1)
                    dve.wait_ge(p_ssq, k + 1)
                    rsqrt(p_newton, k, ssq[:, :], rnorm[:, :], rtmp[:, :], rtmp2[:, :])
                    flat = rows.rearrange("p s h n -> p (s h) n")
                    dve.tensor_tensor(flat, flat, rnorm[:, :].unsqueeze(2).to_broadcast([128, 2 * H, 128]), ALU.mult
                                      ).then_inc(p_unit, 1)

                def am(c):
                    if c == 0:
                        dve.wait_ge(p_dexp, b * 8 + 8)
                    for g in range(H // 2):
                        u = slice(H * c + 2 * g, H * c + 2 * g + 2)
                        dve.wait_ge(p_kq, b * 16 + 4 * c + g + 1)
                        prod = heads(bank[6 + g % 2])
                        dve.tensor_tensor(R[:, u, :], prod[:, 0:2, :], MT[:, u, :], ALU.mult)
                        dve.tensor_tensor(MT[:, u, :], prod[:, 2:4, :], MT[:, u, :], ALU.mult).then_inc(p_am, 1)

                unit(0), unit(1), am(0), unit(2), am(1), unit(3), am(2), am(3)

            def M(b):
                dve.wait_ge(s_xa, b * NC + NC)
                layernorm(ln_m, b, xa, xn)
                dve.wait_ge(m_xab2, b + 1)
                if not isinstance(b, int) or b > 0:
                    dve.wait_ge(st_out, b * 16)
                for c in range(NC):
                    dve.wait_ge(m_down, b * NC + c + 1)
                    last = dve.tensor_tensor(x2[:, c, :], bank[4 + c][:, 0:D], x1m[:, c, :], ALU.add)
                last.then_inc(m_x2, 1)
                dve.wait_ge(m_x2, b + 1)

            def move(b):
                dve.tensor_copy(xa[:, :, :], n0[:, :, :])
                dve.tensor_copy(x1m[:, :, :], x1[:, :, :]).then_inc(x1_moved, 1)

            def S(b):
                for hf in range(2):
                    u = slice(16 * hf, 16 * hf + 16)
                    dve.wait_ge(j_p32, b * 4 + 2 * hf + 1)
                    dve.tensor_scalar(pneg32[32:64, u, :], bank[0 + hf][32:64, :].rearrange("p (u n) -> p u n", u=16),
                                      -1.0, None, ALU.mult).then_inc(j_p32c0, 1)
                for hf in range(2):
                    u = slice(16 * hf, 16 * hf + 16)
                    dve.wait_ge(j_r01, b * 2 + hf + 1)
                    dve.tensor_copy(R[0:32, u, 32:64], bank[6 + hf][0:32, :].rearrange("p (u n) -> p u n", u=16)
                                    ).then_inc(j_r01c, 1)
                for q in (0, 2):
                    u = slice(8 * q, 8 * q + 8)
                    dve.wait_ge(j_p64, b * 4 + q + 1)
                    dve.tensor_scalar(pneg64[64:128, u, :], bank[2 + q][64:128, :].rearrange("p (u n) -> p u n", u=8),
                                      -1.0, None, ALU.mult).then_inc(j_p64v, 1)
                for q in (0, 2):
                    u = slice(8 * q, 8 * q + 8)
                    dve.wait_ge(j_r, b * 4 + q + 1)
                    dve.tensor_copy(R[0:64, u, 64:128], bank[(6 + q) % 8][0:64, :].rearrange("p (u n) -> p u n", u=8)
                                    ).then_inc(j_rv, 1)
                for c in range(NC):
                    if c > 0:
                        for g in range(2):
                            dve.wait_ge(s_ks, b * 6 + 2 * (c - 1) + g + 1)
                            for h in range(4):
                                u = H * c + 4 * g + h
                                last = dve.scalar_tensor_tensor(out=V[:, u, :], in0=heads(bank[2 + g])[:, h, :],
                                                                scalar=egn[:, u:u + 1], in1=V[:, u, :],
                                                                op0=ALU.mult, op1=ALU.add)
                            last.then_inc(s_rhs, 1)
                    if c < NC - 1:
                        for g in range(2):
                            dve.wait_ge(s_up, b * 6 + 2 * c + g + 1)
                            if c == 0:
                                dve.tensor_copy(state[:, 4 * g:4 * g + 4, :], heads(bank[6 + g])).then_inc(s_S, 1)
                            else:
                                dve.wait_ge(s_o, b * 8 + 2 * c + g + 1)
                                for h in range(4):
                                    hh = 4 * g + h
                                    last = dve.scalar_tensor_tensor(out=state[:, hh, :], in0=state[:, hh, :],
                                                                    scalar=egC[:, H * c + hh:H * c + hh + 1],
                                                                    in1=heads(bank[6 + g])[:, h, :],
                                                                    op0=ALU.mult, op1=ALU.add)
                                last.then_inc(s_S, 1)
                    dve.wait_ge(s_y, b * NC + c + 1)
                    if c == 0:
                        dve.wait_ge(x1_moved, b + 1)
                    dve.tensor_tensor(xa[:, c, :], bank[4][:, 0:D], xa[:, c, :], ALU.add).then_inc(s_xa, 1)

            F1(0), N(0), gates(0), P(0)
            move(0)
            F1(1), N(1), gates(1), S(0)
            with dve.Fori(1, B - 1) as t:
                P(t), M(t - 1), move(t), F1(t + 1), N(t + 1), F2(t - 1), gates(t + 1), S(t)
            P(B - 1), M(B - 2), move(B - 1), F2(B - 2), S(B - 1), M(B - 1), F2(B - 1)

        @block.scalar
        def _(act):
            def ffn(n, b):
                f = F[n]
                act.wait_ge(f["tr"], b + 1)
                act.activation(xT[:, :], bank[0][:, :], ACT.Copy).then_inc(f["xT"], 1)
                for o in range(KB):
                    act.wait_ge(f["gate"], b * 2 * KB + 2 * o + 1)
                    if o >= 2:
                        act.wait_ge(f["hid"], b * KB + o - 1)
                    act.activation(sg[:, o % 2, :], bank[2 * (o % 2)][:, :], ACT.Silu, scale=s1[:, o:o + 1]
                                   ).then_inc(f["silu"], 1)
                for o in range(KB):
                    act.wait_ge(f["l2"], b * KB + o + 1)
                    act.activation(hid[1][:, o, :], bank[4 + o][:, :], ACT.Gelu, scale=sh1[:, o:o + 1]).then_inc(f["g2"], 1)
                for o in range(KB):
                    act.wait_ge(f["l3"], b * KB + o + 1)
                    act.activation(hid[0][:, o, :], bank[o][:, :], ACT.Gelu, scale=sh2[:, o:o + 1]).then_inc(f["g3"], 1)

            def F1(b):
                ffn("f1", b)

            def F2(b):
                ffn("f2", b)

            def N(b):
                act.wait_ge(n_tr, b + 1)
                act.activation(nT[:, :], bank[0][:, :], ACT.Identity, scale=ln1w, bias=ln1b).then_inc(n_nT, 1)
                act.wait_ge(n_abs, b * 2 + 2)
                act.activation(ez[:, :], absz[:, :], ACT.Exp, scale=-1.0).then_inc(n_exp, 1)
                act.wait_ge(n_exp, b + 1)
                act.activation(lz[:, :], ez[:, :], ACT.Ln, bias=1.0).then_inc(n_ln, 1)

            def P(b):
                act.wait_ge(p_g, b + 1)
                act.wait_ge(p_kdl, b + 1)
                act.activation(eg[:, :], bank[1][:, 0:U], ACT.Exp)
                act.activation(egC[:, :], bank[1][:, U:2 * U], ACT.Exp).then_inc(p_gexp, 1)
                act.activation(kds[:, :], kdl[:, :], ACT.Exp).then_inc(p_kds, 1)
                for q in range(8):
                    act.wait_ge(p_d, b * 8 + q + 1)
                    for h in range(4):
                        u = 4 * q + h
                        last = act.activation(MT[:, u, :], heads(bank[4 + q % 4])[:, h, :], ACT.Exp, bias=biasj[:, u:u + 1])
                    last.then_inc(p_dexp, 1)

                def silus(c):
                    for i in range(6):
                        n = 6 * c + i
                        act.wait_ge(p_proj, b * 6 * NC + n + 1)
                        dst = (qk[c % 2][:, i // 2, 4 * (i % 2):4 * (i % 2) + 4, :] if i < 4
                               else V[:, H * c + 4 * (i - 4):H * c + 4 * (i - 4) + 4, :])
                        act.activation(dst, heads(bank[n % 4]), ACT.Silu).then_inc(p_silu, 1)

                def copies(c):
                    for i in range(6):
                        n = 6 * c + i
                        g = slice(4 * (i % 2), 4 * (i % 2) + 4)
                        gu = slice(H * c + 4 * (i % 2), H * c + 4 * (i % 2) + 4)
                        act.wait_ge(p_tr, b * 6 * NC + n + 1)
                        act.activation((KT[:, gu, :], qT[:, g, :], QET[:, gu, :])[i // 2], heads(bank[4 + n % 2]), ACT.Copy
                                       ).then_inc(p_trc, 1)

                silus(0), silus(1), copies(0), silus(2), copies(1), silus(3), copies(2), copies(3)

            def M(b):
                act.wait_ge(m_tr, b + 1)
                act.activation(xT[:, :], bank[0][:, :], ACT.Identity, scale=ln2w, bias=ln2b).then_inc(m_xT, 1)
                for o in range(KB):
                    act.wait_ge(m_up, b * KB + o + 1)
                    act.activation(hid[1][:, o, :], bank[o][:, :], ACT.Gelu, bias=b1[:, o:o + 1]).then_inc(m_gelu, 1)

            def S(b):
                for hf in range(2):
                    u = slice(16 * hf, 16 * hf + 16)
                    act.wait_ge(j_p32, b * 4 + 2 * hf + 2)
                    act.activation(pneg32[96:128, u, :], bank[2 + hf][96:128, :].rearrange("p (u n) -> p u n", u=16),
                                   ACT.Copy, scale=-1.0).then_inc(j_p32c1, 1)
                for hf in range(2):
                    u = slice(16 * hf, 16 * hf + 16)
                    act.wait_ge(j_t, b * 2 + hf + 1)
                    act.activation(TB[32:64, u, 0:32], bank[4 + hf][32:64, :].rearrange("p (u n) -> p u n", u=16),
                                   ACT.Copy).then_inc(j_tc, 1)
                for hf in range(2):
                    u = slice(16 * hf, 16 * hf + 16)
                    act.wait_ge(j_r23, b * 2 + hf + 1)
                    act.activation(R[64:96, u, 96:128], bank[0 + hf][64:96, :].rearrange("p (u n) -> p u n", u=16),
                                   ACT.Copy).then_inc(j_r23c, 1)
                for q in (1, 3):
                    u = slice(8 * q, 8 * q + 8)
                    act.wait_ge(j_p64, b * 4 + q + 1)
                    act.activation(pneg64[64:128, u, :], bank[2 + q][64:128, :].rearrange("p (u n) -> p u n", u=8),
                                   ACT.Copy, scale=-1.0).then_inc(j_p64a, 1)
                for q in (1, 3):
                    u = slice(8 * q, 8 * q + 8)
                    act.wait_ge(j_r, b * 4 + q + 1)
                    act.activation(R[0:64, u, 64:128], bank[(6 + q) % 8][0:64, :].rearrange("p (u n) -> p u n", u=8),
                                   ACT.Copy).then_inc(j_ra, 1)
                for c in range(NC):
                    for g in range(2):
                        u = slice(H * c + 4 * g, H * c + 4 * g + 4)
                        act.wait_ge(s_w, b * 8 + 2 * c + g + 1)
                        act.activation(V[:, u, :], heads(bank[4 + g]), ACT.Copy).then_inc(s_wc, 1)
                    for g in range(2):
                        act.wait_ge(s_o, b * 8 + 2 * c + g + 1)
                        act.activation(oT[:, 4 * g:4 * g + 4, :], heads(bank[g]), ACT.Copy).then_inc(s_oc, 1)

            act.wait_ge(ld_w, 8 * 16)
            F1(0), N(0), P(0), F1(1), N(1), S(0)
            with act.Fori(1, B - 1) as t:
                P(t), M(t - 1), F1(t + 1), F2(t - 1), N(t + 1), S(t)
            P(B - 1), M(B - 2), F2(B - 2), S(B - 1), M(B - 1), F2(B - 1)

        @block.tensor
        def _(pe):
            def transposes(rows, done):
                for c in range(NC):
                    last = pe.transpose(bank[0][:, 128 * c:128 * c + 128], rows[:, c, :], ident[:, :])
                last.then_inc(done, 1)

            def layer(w, src, banks, ready, first, done):
                for k in range(KB):
                    pe.wait_ge(ready, first + k + 1)
                    for o in range(KB):
                        last = pe.matmul(bank[banks + o][:, :], w[:, k, 128 * o:128 * o + 128], src[:, k, :],
                                         start=(k == 0), stop=(k == KB - 1))
                        if k == KB - 1:
                            last.then_inc(done, 1)

            def down(w, src, ready, first, done):
                for k in range(KB):
                    pe.wait_ge(ready, first + k + 1)
                    for c in range(NC):
                        last = pe.matmul(bank[4 + c][:, 0:D], src[:, k, 128 * c:128 * c + 128], w[:, k, :],
                                         start=(k == 0), stop=(k == KB - 1))
                        if k == KB - 1:
                            last.then_inc(done, 1)

            def ffn(n, b):
                f = F[n]
                pe.wait_ge(ln_f[n].rows, b + 1)
                transposes(xn, f["tr"])
                pe.wait_ge(f["xT"], b + 1)
                for o in range(KB):
                    if o >= 2:
                        pe.wait_ge(f["hid"], b * KB + o - 1)
                    for w, bk in ((w1, 2 * (o % 2)), (w2, 2 * (o % 2) + 1)):
                        pe.matmul(bank[bk][:, :], w[:, 128 * o:128 * o + 128], xT[:, :], start=True, stop=True
                                  ).then_inc(f["gate"], 1)
                return f

            def ffn_rest(f, b):
                layer(h1, hid[0], 4, f["hid"], b * KB, f["l2"])
                layer(h2, hid[1], 0, f["g2"], b * KB, f["l3"])
                down(w3, hid[0], f["g3"], b * KB, f["l4"])

            def F1(b):
                if isinstance(b, int) and b == 1:
                    pe.wait_ge(p_silu, 6 * NC)
                f = ffn("f1", b)
                if isinstance(b, int) and b == 1:
                    pe.wait_ge(p_trc, 6 * NC)
                    pe.wait_ge(p_am, 16)
                elif not isinstance(b, int):
                    pe.wait_ge(m_x2, b - 1)
                ffn_rest(f, b)

            def F2(b):
                f = ffn("f2", b)
                if isinstance(b, int):
                    pe.wait_ge(m_x2, b + 1)
                else:
                    pe.wait_ge(F["f1"]["res"], b + 3)
                ffn_rest(f, b)

            def N(b):
                pe.wait_ge(ln_n1.rows, b + 1)
                transposes(xn1, n_tr)
                pe.wait_ge(n_nT, b + 1)
                for c in range(NC):
                    last = pe.matmul(bank[1][:, 16 * c:16 * c + 16], nT[:, 128 * c:128 * c + 128], wba[:, :],
                                     start=True, stop=True)
                last.then_inc(n_logit, 1)

            def P(b):
                pe.wait_ge(n_lo, b + 1)
                pe.matmul(bank[1][:, 0:U], triu[:, :], lga[:, :], start=True, stop=True)
                pe.matmul(bank[1][:, U:2 * U], ones[:, :].to_broadcast([128, 128]), lga[:, :], start=True, stop=True).then_inc(p_g, 1)
                if not isinstance(b, int) or b > 0:
                    pe.wait_ge(s_xa, b * NC)
                else:
                    pe.wait_ge(F["f1"]["res"], 1)
                for q in range(8):
                    bk = bank[4 + q % 4]
                    if q >= 4:
                        pe.wait_ge(p_dexp, b * 8 + q - 3)
                    pe.matmul(bk[:, :], identb[:, :], maskb[:, :].unsqueeze(1).to_broadcast([128, 4, 128]),
                              start=True, stop=False, skip_group_check=True)
                    for h in range(4):
                        u = 4 * q + h
                        for part in (lah, lal):
                            last = pe.matmul(heads(bk)[:, h, :], part[:, u:u + 1].to_broadcast([128, 128]), triur[:, :],
                                             start=False, stop=(part is lal and h == 3), skip_group_check=True)
                    last.then_inc(p_d, 1)

                def proj(c):
                    if c == 0:
                        pe.wait_ge(p_kds, b + 1)
                    for i in range(6):
                        n = 6 * c + i
                        if n >= 4:
                            pe.wait_ge(p_silu, b * 6 * NC + n - 3)
                        pe.matmul(bank[n % 4][:, :], nT[:, 128 * c:128 * c + 128],
                                  wqkv[:, i // 2, 512 * (i % 2):512 * (i % 2) + 512], start=True, stop=True
                                  ).then_inc(p_proj, 1)

                def kq(c):
                    if c == 0:
                        pe.wait_ge(p_dexp, b * 8 + 8)
                    for i in range(6):
                        n = 6 * c + i
                        if i == 0:
                            pe.wait_ge(p_unit, b * NC + c + 1)
                        if i == 4:
                            pe.wait_ge(p_qe, b * NC + c + 1)
                        if n >= 2:
                            pe.wait_ge(p_trc, b * 6 * NC + n - 1)
                        for h in range(4):
                            hh = 4 * (i % 2) + h
                            src = (qk[c % 2][:, 1, hh, :], qk[c % 2][:, 0, hh, :], qe[:, hh, :])[i // 2]
                            last = pe.transpose(bank[4 + n % 2][:, 128 * h:128 * h + 128], src, ident[:, :])
                        last.then_inc(p_tr, 1)
                    pe.wait_ge(p_trc, b * 6 * NC + 6 * c + 4)
                    for g in range(H // 2):
                        m = 4 * c + g
                        if m >= 2:
                            pe.wait_ge(p_am, b * 16 + m - 1)
                        for i in range(2):
                            u = H * c + 2 * g + i
                            pe.matmul(bank[6 + g % 2][:, 128 * i:128 * i + 128], KT[:, u, :], KT[:, u, :],
                                      start=True, stop=True)
                            last = pe.matmul(bank[6 + g % 2][:, 256 + 128 * i:384 + 128 * i], KT[:, u, :],
                                             qT[:, 2 * g + i, :], start=True, stop=True)
                        last.then_inc(p_kq, 1)

                proj(0), proj(1), kq(0), proj(2), kq(1), proj(3), kq(2), kq(3)

            def M(b):
                pe.wait_ge(ln_m.rows, b + 1)
                if isinstance(b, int) and b == B - 1:
                    pass
                else:
                    pe.wait_ge(p_silu, b * 6 * NC + 12 * NC)
                transposes(xn, m_tr)
                pe.wait_ge(m_xT, b + 1)
                for o in range(KB):
                    pe.matmul(bank[o][:, :], wm1[:, 128 * o:128 * o + 128], xT[:, :], start=True, stop=True
                              ).then_inc(m_up, 1)
                if isinstance(b, int) and b == B - 1:
                    pe.wait_ge(s_xa, B * NC)
                else:
                    pe.wait_ge(p_am, b * 16 + 32)
                    pe.wait_ge(p_trc, b * 6 * NC + 12 * NC)
                down(wm2, hid[1], m_gelu, b * KB, m_down)

            def hold(bk):
                pe.matmul(bk[:, 0:1], ident[:, :], ident[:, 0:1], start=True, stop=True)

            def S(b):
                pe.wait_ge(b_load, b * 7 * 16 + 7 * 16)
                if isinstance(b, int) and b == 0:
                    pe.wait_ge(F["f1"]["res"], 2)
                    pe.wait_ge(n_lg, 2)
                elif isinstance(b, int):
                    pe.wait_ge(F["f2"]["res"], b)
                else:
                    pe.wait_ge(F["f2"]["res"], b)
                    pe.wait_ge(n_lg, b + 2)
                hold(bank[0])
                for hf in range(2):
                    for pair in range(2):
                        e, o = 64 * pair, 64 * pair + 32
                        for i in range(16):
                            u = 16 * hf + i
                            last = pe.matmul(bank[2 * pair + hf][o:o + 32, 32 * i:32 * i + 32],
                                             R[e:e + 32, u, o:o + 32], TB[e:e + 32, u, 0:32], start=True, stop=True)
                        last.then_inc(j_p32, 1)
                for hf in range(2):
                    pe.wait_ge(j_p32c0, b * 2 + hf + 1)
                    hold(bank[4 + hf])
                    for i in range(16):
                        u = 16 * hf + i
                        last = pe.matmul(bank[4 + hf][32:64, 32 * i:32 * i + 32], R[32:64, u, 32:64],
                                         pneg32[32:64, u, :], start=True, stop=True)
                    last.then_inc(j_t, 1)
                for pair, bks, done in ((0, (6, 7), j_r01), (1, (0, 1), j_r23)):
                    e, o = 64 * pair, 64 * pair + 32
                    for hf in range(2):
                        if pair == 1:
                            pe.wait_ge(j_p32c1, b * 2 + hf + 1)
                            hold(bank[hf])
                        for i in range(16):
                            u = 16 * hf + i
                            last = pe.matmul(bank[bks[hf]][e:e + 32, 32 * i:32 * i + 32], pneg32[o:o + 32, u, :],
                                             R[o:o + 32, u, o:o + 32], start=True, stop=True)
                        last.then_inc(done, 1)
                pe.wait_ge(j_tc, b * 2 + 2)
                hold(bank[2])
                for q in range(4):
                    for i in range(8):
                        u = 8 * q + i
                        last = pe.matmul(bank[2 + q][64:128, 64 * i:64 * i + 64], R[0:64, u, 64:128], TB[0:64, u, :],
                                         start=True, stop=True)
                    last.then_inc(j_p64, 1)
                pe.wait_ge(j_r23c, b * 2 + 2)
                pe.wait_ge(j_r01c, b * 2 + 2)
                for q in range(4):
                    pe.wait_ge((j_p64v, j_p64a)[q % 2], b * 2 + q // 2 + 1)
                    hold(bank[(6 + q) % 8])
                    for i in range(8):
                        u = 8 * q + i
                        last = pe.matmul(bank[(6 + q) % 8][0:64, 64 * i:64 * i + 64], pneg64[64:128, u, :],
                                         R[64:128, u, 64:128], start=True, stop=True)
                    last.then_inc(j_r, 1)
                pe.wait_ge(j_rv, b * 2 + 2)
                pe.wait_ge(j_ra, b * 2 + 2)

                for c in range(NC):
                    if c > 0:
                        for g in range(2):
                            pe.wait_ge(s_S, b * 6 + 2 * (c - 1) + g + 1)
                            for h in range(4):
                                u = H * c + 4 * g + h
                                last = pe.matmul(heads(bank[2 + g])[:, h, :], KT[:, u, :], state[:, 4 * g + h, :],
                                                 start=True, stop=True)
                            last.then_inc(s_ks, 1)
                    for g in range(2):
                        if c > 0:
                            pe.wait_ge(s_rhs, b * 6 + 2 * (c - 1) + g + 1)
                            if g == 0:
                                pe.wait_ge(s_xa, b * NC + c)
                        for h in range(4):
                            u = H * c + 4 * g + h
                            last = pe.matmul(heads(bank[4 + g])[:, h, :], R[:, u, :], V[:, u, :], start=True, stop=True)
                        last.then_inc(s_w, 1)
                    for g in range(2):
                        pe.wait_ge(s_wc, b * 8 + 2 * c + g + 1)
                        if c < NC - 1:
                            for h in range(4):
                                u = H * c + 4 * g + h
                                last = pe.matmul(heads(bank[6 + g])[:, h, :], KD[:, u, :], V[:, u, :], start=True, stop=True)
                            last.then_inc(s_up, 1)
                        for h in range(4):
                            u = H * c + 4 * g + h
                            last = pe.matmul(heads(bank[g])[:, h, :], V[:, u, :], MT[:, u, :], start=True, stop=(c == 0))
                            if c > 0:
                                last = pe.matmul(heads(bank[g])[:, h, :], state[:, 4 * g + h, :], QET[:, u, :],
                                                 start=False, stop=True)
                        last.then_inc(s_o, 1)
                    for g in range(2):
                        pe.wait_ge(s_oc, b * 8 + 2 * c + g + 1)
                        for h in range(4):
                            hh = 4 * g + h
                            last = pe.matmul(bank[4][:, 0:D], oT[:, hh, :], wo[:, hh, :], start=(hh == 0), stop=(hh == H - 1))
                    last.then_inc(s_y, 1)

            pe.wait_ge(c_pool, 1)
            pe.wait_ge(c_dve, 1)
            pe.wait_ge(ld_w, 8 * 16)
            F1(0)
            pe.wait_ge(ld_a, 8 * 16)
            N(0), P(0), F1(1), N(1), S(0)
            with pe.Fori(1, B - 1) as t:
                P(t), M(t - 1), F1(t + 1), F2(t - 1), N(t + 1), S(t)
            P(B - 1), M(B - 2), F2(B - 2), S(B - 1), M(B - 1), F2(B - 1)


def kernel(**inputs):
    import numpy as np
    import concourse.bacc as bacc
    from concourse.bass_utils import run_bass_kernel_spmd

    a = {k: np.asarray(v) for k, v in inputs.items()}
    at, ff = "L0_attn_", "L0_ffn_"

    def column_blocks(v):
        return v.reshape(KB, 128).T

    cols = [column_blocks(a[ff + k]) for k in ("w1_s", "w2_s", "h1_s", "h2_s")] + [column_blocks(a[at + "b1"])]
    cols += [a[at + k].reshape(128, 1) for k in ("ln1_w", "ln1_b", "ln2_w", "ln2_b")]
    host = {
        "x": a[at + "x"], "w1T": a[ff + "w1_w"].T, "w2T": a[ff + "w2_w"].T, "h1T": a[ff + "h1_w"].T,
        "h2T": a[ff + "h2_w"].T, "w3T": a[ff + "w3_w"].T, "s3": a[ff + "w3_s"], "b2": a[at + "b2"],
        "cols": np.concatenate(cols, axis=1),
    }
    host.update({k: a[at + k] for k in ("Wq", "Wk", "Wv", "Wb", "Wa", "Wo", "W1", "W2")})

    nc = bacc.Bacc("TRN2", target_bir_lowering=False, num_devices=1)
    arrays, aps = {}, {}
    for name, v in host.items():
        arrays["in_" + name] = np.ascontiguousarray(v)
        aps[name] = nc.dram_tensor("in_" + name, v.shape, mybir.dt.from_np(v.dtype), kind="ExternalInput").ap()
    aps["out"] = nc.dram_tensor("out_x", (B, T, D), mybir.dt.float32, kind="ExternalOutput").ap()
    build_program(nc, aps)
    r = run_bass_kernel_spmd(nc, [arrays], core_ids=[0])
    return r.results[0]["out_x"]
```

```python
from contextlib import ExitStack

import concourse.bass as bass
from concourse import mybir

B, T, D, H, HID = 8, 512, 128, 8, 512
C = 128
NC = T // C
U = NC * H
KB = HID // 128
BS = 32
NBLK = C // BS
EPS_LN, EPS_L2 = 1e-5, 1e-6
NEG = -1e30
RSQRT_STEPS = 11
FFN_SLOTS = 5 * KB


def build_program(nc, d):
    f32, f32r, bf16, i32 = mybir.dt.float32, mybir.dt.float32r, mybir.dt.bfloat16, mybir.dt.int32
    ALU, ACT, AX = mybir.AluOpType, mybir.ActivationFunctionType, mybir.AxisListType
    ctx = ExitStack()
    with ctx:
        def sb(name, shape, dt=f32):
            return ctx.enter_context(nc.sbuf_tensor(name, shape, dt))

        def sem(name):
            return ctx.enter_context(nc.semaphore(name))

        w1 = sb("w1", [128, HID])
        w2 = sb("w2", [128, HID])
        h1 = sb("h1", [128, KB, HID])
        h2 = sb("h2", [128, KB, HID])
        w3 = sb("w3", [128, KB, D])
        wqkv = sb("wqkv", [128, 3, H * 128])
        wba = sb("wba", [128, 2 * H])
        wo = sb("wo", [128, H, D])
        wm1 = sb("wm1", [128, HID])
        wm2 = sb("wm2", [128, KB, D])
        cols = sb("cols", [128, 24])
        s1, s2, sh1, sh2, b1 = (cols[:, 4 * i:4 * i + 4] for i in range(5))
        ln1w, ln1b, ln2w, ln2b = (cols[:, 20 + i:21 + i] for i in range(4))
        s3row = sb("s3row", [128, D])
        b2row = sb("b2row", [128, D])

        ident = sb("ident", [128, 128])
        identb = sb("identb", [128, 128], bf16)
        triu = sb("triu", [128, 128])
        triur = sb("triur", [128, 128], f32r)
        ones = sb("ones", [128, 1])
        maskb = sb("maskb", [128, 128], bf16)

        xin = sb("xin", [128, NC, D])
        x1 = sb("x1", [128, NC, D])
        x1m = sb("x1m", [128, NC, D])
        x2 = sb("x2", [128, NC, D])
        n0 = sb("n0", [128, NC, D])
        xa = sb("xa", [128, NC, D])
        rows_or_qe = sb("rows_or_qe", [128, 2 * T])
        xn = rows_or_qe[:, 0:T].rearrange("p (c n) -> p c n", c=NC)
        xn1 = rows_or_qe[:, T:].rearrange("p (c n) -> p c n", c=NC)
        qe = rows_or_qe[:, :].rearrange("p (h n) -> p h n", h=H)
        xT = sb("xT", [128, T])
        nT = sb("nT", [128, T])

        big = [sb("big0", [128, 2 * H * 128]), sb("big1", [128, 2 * H * 128])]
        hid = [t[:, :].rearrange("p (k n) -> p k n", k=KB) for t in big]
        qk = [t[:, :].rearrange("p (s h n) -> p s h n", s=2, h=H) for t in big]
        mid = sb("mid", [128, H * 128])
        sg = mid[:, :].rearrange("p (s n) -> p s n", s=2)
        qT = mid[:, :].rearrange("p (h n) -> p h n", h=H)
        oT = qT

        V = sb("V", [128, U, 128])
        KD = sb("KD", [128, U, 128])
        KT = sb("KT", [128, U, 128])
        QET = sb("QET", [128, U, 128])
        R = sb("R", [128, U, 128])
        MT = sb("MT", [128, U, 128])
        TB = sb("TB", [128, U, 64])
        state = sb("state", [128, H, 128])
        blkA = sb("blkA", [128, BS * BS])
        blkT = sb("blkT", [128, BS * BS])
        blkP = sb("blkP", [128, 256])

        absz = sb("absz", [128, NC * 2 * H])
        ez = sb("ez", [128, NC * 2 * H])
        lz = sb("lz", [128, NC * 2 * H])
        lgb = sb("lgb", [128, U])
        lga = sb("lga", [128, U])
        lah = sb("lah", [128, U], f32r)
        lal = sb("lal", [128, U], f32r)
        gn = sb("gn", [128, 2 * U])
        biasj = sb("biasj", [128, U])
        kdl = sb("kdl", [128, U])
        kds = sb("kds", [128, U])
        eg = sb("eg", [128, U])
        egn = sb("egn", [128, U])
        egC = sb("egC", [128, U])
        bst = sb("bst", [128, 2 * H, 6])
        bsq = sb("bsq", [128, 2 * H, 2])
        bss = sb("bss", [128, 2 * H, 2])
        ssq = sb("ssq", [128, 2 * H])
        rnorm = sb("rnorm", [128, 2 * H])
        mhalf = sb("mhalf", [128, 1])

        bank = [ctx.enter_context(nc.psum_tensor(f"bank{i}", [128, 512], f32)) for i in range(8)]

        def heads(bk):
            return bk[:, :].rearrange("p (h n) -> p h n", h=4)

        blocks_out = nc.dram_tensor("blocks_out", [NBLK, U, BS, BS], f32).ap()
        t_back = nc.dram_tensor("t_back", [NBLK, U, BS, BS], f32).ap()
        r_back = nc.dram_tensor("r_back", [NBLK, U, BS, BS], f32).ap()

        ld_x = sem("ld_x")
        ld_w = sem("ld_w")
        ld_a = sem("ld_a")
        c_mem = sem("c_mem")
        c_pool = sem("c_pool")
        c_dve = sem("c_dve")
        st_out = sem("st_out")

        class Site:
            def __init__(self, n):
                self.stats, self.aggr, self.var = sem(n + "_stats"), sem(n + "_aggr"), sem(n + "_var")
                self.sq, self.newton, self.rows = sem(n + "_sq"), sem(n + "_newton"), sem(n + "_rows")
                self.st, self.mean = sb(n + "_st", [128, NC, 6]), sb(n + "_mean", [128, NC])
                self.ve, self.rs = sb(n + "_ve", [128, NC]), sb(n + "_rs", [128, NC])
                self.ta, self.tb = sb(n + "_ta", [128, NC]), sb(n + "_tb", [128, NC])

        ln_f = {"f1": Site("lnf1"), "f2": Site("lnf2")}
        ln_m, ln_n0, ln_n1 = Site("lnm"), Site("lnn0"), Site("lnn1")

        def ffn_sems(n):
            names = ("tr", "xT", "gate", "silu", "hid", "l2", "g2", "l3", "g3", "l4", "sc", "res")
            return {k: sem(f"{n}_{k}") for k in names}

        F = {"f1": ffn_sems("f1"), "f2": ffn_sems("f2")}
        ld_x1 = sem("ld_x1")
        x1_moved = sem("x1_moved")
        n_tr, n_nT, n_logit = sem("n_tr"), sem("n_nT"), sem("n_logit")
        n_abs, n_exp, n_ln, n_lg = (sem("n_" + k) for k in ("abs", "exp", "ln", "lg"))
        n_hi, n_lo, n_g, n_gn, n_bias = (sem("n_" + k) for k in ("hi", "lo", "g", "gn", "bias"))
        p_gexp, p_kdl, p_kds, p_egn = (sem("p_" + k) for k in ("gexp", "kdl", "kds", "egn"))
        d_sum, d_exp = sem("d_sum"), sem("d_exp")
        p_proj, p_silu = sem("p_proj"), sem("p_silu")
        p_bst, p_ss1, p_ss2, p_ssq = (sem("p_" + k) for k in ("bst", "ss1", "ss2", "ssq"))
        p_norm = sem("p_norm")
        p_unit, p_kd, p_qe = sem("p_unit"), sem("p_kd"), sem("p_qe")
        p_tr, p_trc = sem("p_tr"), sem("p_trc")
        p_kq, p_am = sem("p_kq"), sem("p_am")
        b_out, b_in = sem("b_out"), sem("b_in")
        b_init, b_prod, b_R = sem("b_init"), sem("b_prod"), sem("b_R")
        b_back, b_load = sem("b_back"), sem("b_load")
        j_full, j_dve, j_act = sem("j_full"), sem("j_dve"), sem("j_act")
        s_ks, s_rhs = sem("s_ks"), sem("s_rhs")
        s_w, s_wc = sem("s_w"), sem("s_wc")
        s_up, s_S = sem("s_up"), sem("s_S")
        s_o, s_oc = sem("s_o"), sem("s_oc")
        s_y, s_xa = sem("s_y"), sem("s_xa")
        m_tr, m_xT, m_up, m_gelu, m_down = (sem("m_" + k) for k in ("tr", "xT", "up", "gelu", "down"))
        m_xab, m_xab2, m_x2 = sem("m_xab"), sem("m_xab2"), sem("m_x2")

        JOINS = [("p32", (0, 0)), ("p32", (1, 0)), ("p32", (0, 1)), ("p32", (1, 1)),
                 ("r32", (0, 0)), ("t32", (0, 0)), ("r32", (0, 1)), ("t32", (0, 1)), ("r32", (1, 0)), ("r32", (1, 1)),
                 ("p64", 0), ("p64", 1), ("p64", 2), ("p64", 3), ("r64", 0), ("r64", 1), ("r64", 2), ("r64", 3)]
        NJ = len(JOINS)

        def join_result(n):
            kind, part = JOINS[n]
            bk = bank[6 + n % 2]
            if kind in ("p64", "r64"):
                u = slice(8 * part, 8 * part + 8)
                src = bk[:, :].rearrange("p (u n) -> p u n", u=8)
                return (src[64:128], TB[64:128, u, :], -1.0) if kind == "p64" else (src[0:64], R[0:64, u, 64:128], 1.0)
            pair, half = part
            u = slice(16 * half, 16 * half + 16)
            e, o = slice(64 * pair, 64 * pair + 32), slice(64 * pair + 32, 64 * pair + 64)
            src = bk[:, :].rearrange("p (u n) -> p u n", u=16)
            if kind == "p32":
                return src[o], TB[o, u, 0:32], -1.0
            return (src[o], TB[o, u, 0:32], 1.0) if kind == "t32" else (src[e], R[e, u, o], 1.0)

        block = ctx.enter_context(nc.Block())

        @block.sync
        def _(sp):
            def rows_of(x, b):
                return x[bass.ds(b, 1), :, :].rearrange("o (c p) n -> p (o c) n", p=128)

            def load_xin(b):
                if not isinstance(b, int) or b > 0:
                    sp.wait_ge(F["f1"]["tr"], b)
                sp.dma_start(xin[:, :, :], rows_of(d["x"], b)).then_inc(ld_x, 16)

            def load_x1(b):
                if not isinstance(b, int) or b > 0:
                    sp.wait_ge(x1_moved, b)
                sp.dma_start(x1[:, :, :], rows_of(d["x"], b)).then_inc(ld_x1, 16)

            load_xin(0)
            for dst, src in ((w1[:, :], d["w1T"]), (w2[:, :], d["w2T"]), (cols[:, :], d["cols"]),
                             (h1[:, :, :], d["h1T"].rearrange("(k p) n -> p k n", p=128)),
                             (h2[:, :, :], d["h2T"].rearrange("(k p) n -> p k n", p=128)),
                             (w3[:, :, :], d["w3T"].rearrange("(k p) n -> p k n", p=128)),
                             (s3row[:, :], d["s3"].partition_broadcast(128)),
                             (b2row[:, :], d["b2"].partition_broadcast(128))):
                sp.dma_start(dst, src).then_inc(ld_w, 16)
            load_x1(0)
            for dst, src in ((wba[:, 0:H], d["Wb"]), (wba[:, H:], d["Wa"]),
                             (wqkv[:, 0, :], d["Wq"]), (wqkv[:, 1, :], d["Wk"]), (wqkv[:, 2, :], d["Wv"]),
                             (wo[:, :, :], d["Wo"].rearrange("(h p) n -> p h n", p=128)),
                             (wm1[:, :], d["W1"]),
                             (wm2[:, :, :], d["W2"].rearrange("(k p) n -> p k n", p=128))):
                sp.dma_start(dst, src).then_inc(ld_a, 16)

            def P(b):
                for c in range(NC):
                    sp.wait_ge(p_am, b * 16 + 4 * c + 3)
                    for p in range(NBLK):
                        r = slice(BS * p, BS * p + BS)
                        sp.dma_start(blocks_out[p, H * c:H * c + H, :, :].rearrange("u j i -> j u i"),
                                     R[r, H * c:H * c + H, r]).then_inc(b_out, 16)
                sp.wait_ge(b_out, b * 256 + 256)
                sp.dma_start(blkA[:, :], blocks_out.rearrange("p u j i -> (p u) (j i)")).then_inc(b_in, 16)

            def back(b):
                sp.wait_ge(b_prod, b * 2 * (BS - 1) + 2 * (BS - 1))
                sp.dma_start(t_back.rearrange("p u i c -> (p u) (i c)"), blkT[:, :]).then_inc(b_back, 16)
                sp.wait_ge(b_R, b + 1)
                sp.dma_start(r_back.rearrange("p u c i -> (p u) (c i)"), blkA[:, :]).then_inc(b_back, 16)
                sp.wait_ge(b_back, b * 32 + 32)
                for p in range(NBLK):
                    r = slice(BS * p, BS * p + BS)
                    sp.dma_start(R[r, :, r], r_back[p, :, :, :].rearrange("u c i -> c u i")).then_inc(b_load, 16)
                for p, col in ((0, 0), (1, BS), (2, 0)):
                    sp.dma_start(TB[BS * p:BS * p + BS, :, col:col + BS],
                                 t_back[p, :, :, :].rearrange("u i c -> i u c")).then_inc(b_load, 16)

            def store(b):
                sp.wait_ge(F["f2"]["res"], b + 1)
                sp.dma_start(rows_of(d["out"], b), x2[:, :, :]).then_inc(st_out, 16)

            load_xin(1)
            P(0), load_x1(1), load_xin(2), back(0)
            with sp.Fori(1, B - 2) as t:
                P(t), load_x1(t + 1), load_xin(t + 2), back(t), store(t - 1)
            P(B - 2), load_x1(B - 1), back(B - 2), store(B - 3)
            P(B - 1), back(B - 1), store(B - 2), store(B - 1)
            sp.wait_ge(st_out, B * 16)

        @block.gpsimd
        def _(pool):
            pool.memset(ident[:, :], 0.0)
            pool.memset(triu[:, :], 1.0)
            pool.memset(identb[:, :], 0.0)
            pool.memset(maskb[:, :], 0.0).then_inc(c_mem, 1)
            pool.memset(ones[:, :], 1.0)
            pool.memset(mhalf[:, :], -0.5)
            pool.memset(TB[:, :, :], 0.0)
            pool.wait_ge(c_mem, 1)
            pool.affine_select(out=ident[:, :], in_=ident[:, :], compare_op=ALU.not_equal, fill=1.0,
                               base=0, pattern=[[-1, 128]], channel_multiplier=1)
            pool.affine_select(out=identb[:, :], in_=identb[:, :], compare_op=ALU.not_equal, fill=1.0,
                               base=0, pattern=[[-1, 128]], channel_multiplier=1)
            pool.affine_select(out=triu[:, :], in_=triu[:, :], compare_op=ALU.is_ge, fill=0.0,
                               base=0, pattern=[[1, 128]], channel_multiplier=-1)
            pool.affine_select(out=maskb[:, :], in_=maskb[:, :], compare_op=ALU.is_ge, fill=NEG,
                               base=0, pattern=[[1, 128]], channel_multiplier=-1).then_inc(c_pool, 1)

            def norms(b, c):
                pool.wait_ge(p_ssq, b * NC + c + 1)
                pool.tensor_tensor(rnorm[:, :], ssq[:, :], mhalf[:, :].to_broadcast([128, 2 * H]), ALU.pow
                                   ).then_inc(p_norm, 1)

            def scaled(b, c):
                u = slice(H * c, H * c + H)
                pool.wait_ge(p_unit, b * NC + c + 1)
                if c == 0:
                    pool.wait_ge(p_kds, b + 1)
                    pool.wait_ge(p_gexp, b + 1)
                pool.tensor_tensor(KD[:, u, :], qk[c % 2][:, 1, :, :],
                                   kds[:, u].unsqueeze(2).to_broadcast([128, H, 128]), ALU.mult).then_inc(p_kd, 1)
                if c > 0:
                    pool.wait_ge(p_tr, b * 6 * NC + 6 * c)
                pool.tensor_tensor(qe[:, :, :], qk[c % 2][:, 0, :, :],
                                   eg[:, u].unsqueeze(2).to_broadcast([128, H, 128]), ALU.mult).then_inc(p_qe, 1)

            A3 = blkA[:, :].rearrange("q (j i) -> q j i", j=BS)
            T3 = blkT[:, :].rearrange("q (i c) -> q i c", i=BS)

            def invert(b):
                pool.wait_ge(b_init, b * 2 + 2)
                pool.wait_ge(b_in, b * 16 + 16)
                steps = 2 * (BS - 1)
                for j in range(BS - 1):
                    n, m = BS - 1 - j, j + 1
                    prod = blkP[:, 0:n * m].rearrange("q (i c) -> q i c", i=n)
                    if j > 0:
                        pool.wait_ge(b_prod, b * steps + 2 * j)
                    pool.tensor_tensor(prod, A3[:, j, j + 1:].unsqueeze(2).to_broadcast([128, n, m]),
                                       T3[:, j:j + 1, 0:m].to_broadcast([128, n, m]), ALU.mult).then_inc(b_prod, 1)
                    pool.wait_ge(b_prod, b * steps + 2 * j + 1)
                    pool.tensor_tensor(T3[:, j + 1:, 0:m], T3[:, j + 1:, 0:m], prod, ALU.subtract).then_inc(b_prod, 1)
                pool.wait_ge(b_prod, b * steps + steps)
                pool.tensor_tensor(A3, T3.rearrange("q i c -> q c i"),
                                   ones[:, :].unsqueeze(2).to_broadcast([128, BS, BS]), ALU.mult).then_inc(b_R, 1)

            def M(b):
                pool.wait_ge(s_xa, b * NC + NC)
                pool.wait_ge(x1_moved, b + 1)
                pool.tensor_tensor(x1m[:, :, :], xa[:, :, :], x1m[:, :, :], ALU.add).then_inc(m_xab, 1)
                pool.wait_ge(m_xab, b + 1)
                pool.tensor_tensor(x1m[:, :, :], x1m[:, :, :],
                                   b2row[:, :].unsqueeze(1).to_broadcast([128, NC, D]), ALU.add).then_inc(m_xab2, 1)

            def P(b, with_m):
                norms(b, 0), scaled(b, 0)
                if with_m:
                    M(b - 1)
                for c in range(1, NC):
                    norms(b, c), scaled(b, c)
                invert(b)

            pool.wait_ge(ld_w, 8 * 16)
            P(0, False)
            with pool.Fori(1, B) as t:
                P(t, True)
            M(B - 1)

        @block.vector
        def _(dve):
            dve.wait_ge(c_pool, 1)
            dve.tensor_copy(triur[:, :], triu[:, :])
            dve.wait_ge(ld_w, 8 * 16)
            dve.tensor_scalar(s3row[:, :], s3row[:, :], 0.5, None, ALU.mult).then_inc(c_dve, 1)

            def rsqrt(done, b, x, y, ta, tb):
                n = b * RSQRT_STEPS
                dve.tensor_scalar(ta.bitcast(i32), x.bitcast(i32), 1, None, ALU.arith_shift_right).then_inc(done, 1)
                dve.wait_ge(done, n + 1)
                dve.tensor_scalar(y.bitcast(i32), ta.bitcast(i32), -1, 0x5F3759DF, ALU.mult, ALU.add).then_inc(done, 1)
                for i in range(3):
                    dve.wait_ge(done, n + 3 * i + 2)
                    dve.tensor_tensor(ta, y, y, ALU.mult).then_inc(done, 1)
                    dve.wait_ge(done, n + 3 * i + 3)
                    dve.scalar_tensor_tensor(out=tb, in0=ta, scalar=-0.5, in1=x, op0=ALU.mult, op1=ALU.mult
                                             ).then_inc(done, 1)
                    dve.wait_ge(done, n + 3 * i + 4)
                    dve.scalar_tensor_tensor(out=y, in0=tb, scalar=1.5, in1=y, op0=ALU.add, op1=ALU.mult
                                             ).then_inc(done, 1)
                dve.wait_ge(done, n + RSQRT_STEPS)

            def layernorm(s, b, x, out):
                for c in range(NC):
                    last = dve.bn_stats(s.st[:, c, :], x[:, c, :])
                last.then_inc(s.stats, 1)
                dve.wait_ge(s.stats, b + 1)
                dve.tensor_tensor(s.mean[:, :], s.st[:, :, 1], s.st[:, :, 4], ALU.add)
                dve.tensor_tensor(s.ta[:, :], s.st[:, :, 1], s.st[:, :, 4], ALU.subtract)
                dve.tensor_tensor(s.tb[:, :], s.st[:, :, 2], s.st[:, :, 5], ALU.add).then_inc(s.aggr, 1)
                dve.wait_ge(s.aggr, b + 1)
                dve.tensor_scalar(s.mean[:, :], s.mean[:, :], 0.5, None, ALU.mult)
                dve.tensor_scalar(s.ve[:, :], s.tb[:, :], 1.0 / D, EPS_LN, ALU.mult, ALU.add)
                dve.scalar_tensor_tensor(out=s.ta[:, :], in0=s.ta[:, :], scalar=0.25, in1=s.ta[:, :],
                                         op0=ALU.mult, op1=ALU.mult).then_inc(s.sq, 1)
                dve.wait_ge(s.sq, b + 1)
                dve.tensor_tensor(s.ve[:, :], s.ve[:, :], s.ta[:, :], ALU.add).then_inc(s.var, 1)
                dve.wait_ge(s.var, b + 1)
                rsqrt(s.newton, b, s.ve[:, :], s.rs[:, :], s.ta[:, :], s.tb[:, :])
                for c in range(NC):
                    last = dve.tensor_scalar(out[:, c, :], x[:, c, :], s.mean[:, c:c + 1], s.rs[:, c:c + 1],
                                             ALU.subtract, ALU.mult)
                last.then_inc(s.rows, 1)

            def LN_F1(b):
                dve.wait_ge(ld_x, b * 16 + 16)
                layernorm(ln_f["f1"], b, xin, xin)

            def LN_F2(b):
                dve.wait_ge(m_x2, b + 1)
                layernorm(ln_f["f2"], b, x2, xn)

            def LN_M(b):
                dve.wait_ge(s_xa, b * NC + NC)
                dve.wait_ge(m_xab, b + 1)
                layernorm(ln_m, b, xa, xa)

            def gating(n, b):
                f = F[n]
                for o in range(KB):
                    dve.wait_ge(f["gate"], b * 2 * KB + 2 * o + 2)
                    dve.wait_ge(f["silu"], b * KB + o + 1)
                    dve.scalar_tensor_tensor(out=hid[0][:, o, :], in0=bank[1 + 2 * (o % 2)][:, :], scalar=s2[:, o:o + 1],
                                             in1=sg[:, o % 2, :], op0=ALU.mult, op1=ALU.mult).then_inc(f["hid"], 1)

            def result(n, b, x):
                f = F[n]
                dve.wait_ge(f["l4"], b + 1)
                dve.tensor_tensor(xn[:, :, :], heads(bank[4]), s3row[:, :].unsqueeze(1).to_broadcast([128, NC, D]),
                                  ALU.mult).then_inc(f["sc"], 1)
                dve.wait_ge(f["sc"], b + 1)
                dve.tensor_tensor(x[:, :, :], xn[:, :, :], x[:, :, :], ALU.add).then_inc(f["res"], 1)

            def F1_result(b):
                dve.wait_ge(ld_x1, b * 16 + 16)
                result("f1", b, x1)

            def N0(b):
                dve.wait_ge(F["f1"]["res"], b + 1)
                layernorm(ln_n0, b, x1, n0)

            def N1(b):
                dve.wait_ge(ln_n0.rows, b + 1)
                layernorm(ln_n1, b, n0, xn1)

            def gates(b):
                dve.wait_ge(n_logit, b + 1)
                z = bank[2][:, 0:NC * 2 * H]
                dve.tensor_scalar(lz[:, :], z, -1.0, None, ALU.mult).then_inc(n_abs, 1)
                dve.wait_ge(n_abs, b * 2 + 1)
                dve.tensor_tensor(absz[:, :], z, lz[:, :], ALU.max).then_inc(n_abs, 1)
                dve.wait_ge(n_ln, b + 1)
                z4 = z.rearrange("p (c s h) -> p c s h", c=NC, s=2)
                l4 = lz[:, :].rearrange("p (c s h) -> p c s h", c=NC, s=2)
                for s, dst in ((0, lgb), (1, lga)):
                    last = dve.scalar_tensor_tensor(out=dst[:, :].rearrange("p (c h) -> p c h", c=NC), in0=z4[:, :, s, :],
                                                    scalar=0.0, in1=l4[:, :, s, :], op0=ALU.min, op1=ALU.subtract)
                last.then_inc(n_lg, 1)
                dve.wait_ge(n_lg, b + 1)
                dve.tensor_copy(lah[:, :], lga[:, :]).then_inc(n_hi, 1)
                dve.wait_ge(n_hi, b + 1)
                dve.tensor_tensor(lal[:, :], lga[:, :], lah[:, :].bitcast(f32), ALU.subtract).then_inc(n_lo, 1)

            def cumulated(b):
                dve.wait_ge(n_g, b + 1)
                dve.tensor_copy(gn[:, :], bank[2][:, 2 * U:4 * U]).then_inc(n_gn, 1)
                dve.tensor_tensor(biasj[:, :], lgb[:, :], bank[2][:, 2 * U:3 * U], ALU.subtract).then_inc(n_bias, 1)

            def vectors(b):
                if not isinstance(b, int) or b > 0:
                    dve.wait_ge(b_back, b * 32)
                dve.memset(blkT[:, :], 0.0).then_inc(b_init, 1)
                dve.wait_ge(b_init, b * 2 + 1)
                dve.memset(blkT[:, 0:BS * BS:BS + 1], 1.0).then_inc(b_init, 1)
                dve.wait_ge(n_bias, b + 1)
                dve.tensor_tensor(kdl[:, :], biasj[:, :], gn[:, U:2 * U], ALU.add).then_inc(p_kdl, 1)
                dve.wait_ge(p_gexp, b + 1)
                dve.tensor_scalar(egn[:, :], eg[:, :], -1.0, None, ALU.mult).then_inc(p_egn, 1)

            def squares(b, c):
                dve.wait_ge(p_silu, b * 6 * NC + 6 * c + 4)
                for i in range(2 * H):
                    last = dve.bn_stats(bst[:, i, :], qk[c % 2][:, i // H, i % H, :])
                last.then_inc(p_bst, 1)
                k = b * NC + c
                dve.wait_ge(p_bst, k + 1)
                dve.tensor_tensor(bsq[:, :, :], bst[:, :, 1::3], bst[:, :, 1::3], ALU.mult).then_inc(p_ss1, 1)
                dve.wait_ge(p_ss1, k + 1)
                dve.scalar_tensor_tensor(out=bss[:, :, :], in0=bsq[:, :, :], scalar=64.0, in1=bst[:, :, 2::3],
                                         op0=ALU.mult, op1=ALU.add).then_inc(p_ss2, 1)
                dve.wait_ge(p_ss2, k + 1)
                dve.scalar_tensor_tensor(out=ssq[:, :], in0=bss[:, :, 0], scalar=EPS_L2, in1=bss[:, :, 1],
                                         op0=ALU.add, op1=ALU.add).then_inc(p_ssq, 1)

            def unit(b, c):
                dve.wait_ge(p_norm, b * NC + c + 1)
                flat = qk[c % 2].rearrange("p s h n -> p (s h) n")
                dve.tensor_tensor(flat, flat, rnorm[:, :].unsqueeze(2).to_broadcast([128, 2 * H, 128]), ALU.mult
                                  ).then_inc(p_unit, 1)

            def decayed(b, c):
                dve.wait_ge(d_exp, b * 8 + 2 * c + 2)
                for g in range(2):
                    u = slice(H * c + 4 * g, H * c + 4 * g + 4)
                    dve.wait_ge(p_kq, b * 16 + 4 * c + 2 * g + 1)
                    dve.tensor_tensor(R[:, u, :], heads(bank[6]), MT[:, u, :], ALU.mult).then_inc(p_am, 1)
                    dve.wait_ge(p_kq, b * 16 + 4 * c + 2 * g + 2)
                    dve.tensor_tensor(MT[:, u, :], heads(bank[7]), MT[:, u, :], ALU.mult).then_inc(p_am, 1)

            def P(b, with_m, with_f1):
                squares(b, 1)
                if with_m:
                    LN_M(b - 1)
                unit(b, 1), decayed(b, 0), squares(b, 2)
                if with_f1:
                    LN_F1(b + 1)
                unit(b, 2), decayed(b, 1), squares(b, 3), unit(b, 3), decayed(b, 2), decayed(b, 3)

            def M_result(b):
                dve.wait_ge(m_xab2, b + 1)
                if not isinstance(b, int) or b > 0:
                    dve.wait_ge(st_out, b * 16)
                dve.wait_ge(m_down, b + 1)
                dve.tensor_tensor(x2[:, :, :], heads(bank[4]), x1m[:, :, :], ALU.add).then_inc(m_x2, 1)

            def move(b):
                if not isinstance(b, int) or b > 0:
                    dve.wait_ge(m_x2, b)
                dve.tensor_copy(xa[:, :, :], n0[:, :, :])
                dve.tensor_copy(x1m[:, :, :], x1[:, :, :]).then_inc(x1_moved, 1)

            def J(b):
                for n in range(0, NJ, 2):
                    src, dst, factor = join_result(n)
                    dve.wait_ge(j_full, b * NJ + n + 1)
                    dve.tensor_scalar(dst, src, factor, None, ALU.mult).then_inc(j_dve, 1)

            def S(b, with_next):
                if with_next:
                    gates(b + 1), cumulated(b + 1)
                for c in range(NC):
                    if c > 0:
                        for g in range(2):
                            dve.wait_ge(s_ks, b * 6 + 2 * (c - 1) + g + 1)
                            for h in range(4):
                                u = H * c + 4 * g + h
                                last = dve.scalar_tensor_tensor(out=V[:, u, :], in0=heads(bank[2 + g])[:, h, :],
                                                                scalar=egn[:, u:u + 1], in1=V[:, u, :],
                                                                op0=ALU.mult, op1=ALU.add)
                            last.then_inc(s_rhs, 1)
                    if c < NC - 1:
                        for g in range(2):
                            dve.wait_ge(s_up, b * 6 + 2 * c + g + 1)
                            if c == 0:
                                dve.tensor_copy(state[:, 4 * g:4 * g + 4, :], heads(bank[6 + g])).then_inc(s_S, 1)
                            else:
                                dve.wait_ge(s_o, b * 8 + 2 * c + g + 1)
                                for h in range(4):
                                    hh = 4 * g + h
                                    last = dve.scalar_tensor_tensor(out=state[:, hh, :], in0=state[:, hh, :],
                                                                    scalar=egC[:, H * c + hh:H * c + hh + 1],
                                                                    in1=heads(bank[6 + g])[:, h, :],
                                                                    op0=ALU.mult, op1=ALU.add)
                                last.then_inc(s_S, 1)
                    elif with_next:
                        squares(b + 1, 0)
                    dve.wait_ge(s_y, b * NC + c + 1)
                    if c == 0:
                        dve.wait_ge(x1_moved, b + 1)
                    dve.tensor_tensor(xa[:, c, :], bank[4][:, 0:D], xa[:, c, :], ALU.add).then_inc(s_xa, 1)
                if with_next:
                    vectors(b + 1), unit(b + 1, 0)

            LN_F1(0), gating("f1", 0), F1_result(0), N0(0), N1(0), gates(0), cumulated(0)
            vectors(0), squares(0, 0), unit(0, 0), P(0, False, True), move(0)
            gating("f1", 1), F1_result(1), N0(1), N1(1), J(0), S(0, True)
            with dve.Fori(1, B - 1) as t:
                P(t, True, True), M_result(t - 1), move(t), LN_F2(t - 1), gating("f1", t + 1), F1_result(t + 1)
                N0(t + 1), gating("f2", t - 1), N1(t + 1), J(t), result("f2", t - 1, x2), S(t, True)
            P(B - 1, True, False), M_result(B - 2), move(B - 1), LN_F2(B - 2)
            gating("f2", B - 2), J(B - 1), result("f2", B - 2, x2), S(B - 1, False)
            LN_M(B - 1), M_result(B - 1), LN_F2(B - 1), gating("f2", B - 1), result("f2", B - 1, x2)

        @block.scalar
        def _(act):
            def input_T(n, b):
                act.wait_ge(F[n]["tr"], b + 1)
                act.activation(xT[:, :], bank[0][:, :], ACT.Copy).then_inc(F[n]["xT"], 1)

            def silus_F(n, b):
                f = F[n]
                for o in range(KB):
                    act.wait_ge(f["gate"], b * 2 * KB + 2 * o + 1)
                    if o >= 2:
                        act.wait_ge(f["hid"], b * KB + o - 1)
                    act.activation(sg[:, o % 2, :], bank[2 * (o % 2)][:, :], ACT.Silu, scale=s1[:, o:o + 1]
                                   ).then_inc(f["silu"], 1)

            def gelus2(n, b, pair):
                for i in range(2):
                    o = 2 * pair + i
                    act.wait_ge(F[n]["l2"], b * KB + o + 1)
                    act.activation(hid[1][:, o, :], bank[(4, 0)[pair] + i][:, :], ACT.Gelu, scale=sh1[:, o:o + 1]
                                   ).then_inc(F[n]["g2"], 1)

            def gelus3(n, b, pair):
                for i in range(2):
                    o = 2 * pair + i
                    act.wait_ge(F[n]["l3"], b * KB + o + 1)
                    act.activation(hid[0][:, o, :], bank[(4, 2)[pair] + i][:, :], ACT.Gelu, scale=sh2[:, o:o + 1]
                                   ).then_inc(F[n]["g3"], 1)

            def F1(b):
                silus_F("f1", b)
                gelus2("f1", b, 0), gelus2("f1", b, 1), gelus3("f1", b, 0), gelus3("f1", b, 1)

            def joined(b, n):
                src, dst, factor = join_result(n)
                act.wait_ge(j_full, b * NJ + n + 1)
                act.activation(dst, src, ACT.Copy, scale=factor).then_inc(j_act, 1)

            def N_T(b):
                act.wait_ge(n_tr, b + 1)
                act.activation(nT[:, :], bank[0][:, :], ACT.Identity, scale=ln1w, bias=ln1b).then_inc(n_nT, 1)

            def F2(b, with_join, with_n):
                silus_F("f2", b)
                for s in range(FFN_SLOTS):
                    if s == 3:
                        gelus2("f2", b, 0)
                    if s == 7:
                        gelus2("f2", b, 1)
                    if s == 11:
                        gelus3("f2", b, 0)
                    if s == 15:
                        gelus3("f2", b, 1)
                    n = s - (FFN_SLOTS - NJ)
                    if with_join and n >= 0 and n % 2 == 1:
                        joined(b + 1, n)
                    if s == 15 and with_n:
                        N_T(b + 2)

            def N_logs(b):
                act.wait_ge(n_abs, b * 2 + 2)
                act.activation(ez[:, :], absz[:, :], ACT.Exp, scale=-1.0).then_inc(n_exp, 1)
                act.wait_ge(n_exp, b + 1)
                act.activation(lz[:, :], ez[:, :], ACT.Ln, bias=1.0).then_inc(n_ln, 1)

            def decays(b, q):
                if q == 0:
                    act.wait_ge(n_bias, b + 1)
                act.wait_ge(d_sum, b * 8 + q + 1)
                for h in range(4):
                    u = 4 * q + h
                    last = act.activation(MT[:, u, :], heads(bank[2 + q % 2])[:, h, :], ACT.Exp, bias=biasj[:, u:u + 1])
                last.then_inc(d_exp, 1)

            def exps(b):
                act.wait_ge(n_gn, b + 1)
                if not isinstance(b, int) or b > 0:
                    act.wait_ge(s_S, b * 6)
                act.activation(eg[:, :], gn[:, 0:U], ACT.Exp)
                act.activation(egC[:, :], gn[:, U:2 * U], ACT.Exp).then_inc(p_gexp, 1)
                act.wait_ge(p_kdl, b + 1)
                act.activation(kds[:, :], kdl[:, :], ACT.Exp).then_inc(p_kds, 1)

            def silu(b, c, i):
                n = 6 * c + i
                bk = bank[6 + n % 2] if n < 4 else bank[n % 4]
                act.wait_ge(p_proj, b * 6 * NC + n + 1)
                dst = (qk[c % 2][:, i // 2, 4 * (i % 2):4 * (i % 2) + 4, :] if i < 4
                       else V[:, H * c + 4 * (i - 4):H * c + 4 * (i - 4) + 4, :])
                act.activation(dst, heads(bk), ACT.Silu).then_inc(p_silu, 1)

            def copy_T(b, c, i):
                n = 6 * c + i
                g = slice(4 * (i % 2), 4 * (i % 2) + 4)
                gu = slice(H * c + 4 * (i % 2), H * c + 4 * (i % 2) + 4)
                act.wait_ge(p_tr, b * 6 * NC + n + 1)
                act.activation((KT[:, gu, :], qT[:, g, :], QET[:, gu, :])[i // 2], heads(bank[4 + n % 2]), ACT.Copy
                               ).then_inc(p_trc, 1)

            def P(b, with_m, with_f1):
                silu(b, 0, 4), silu(b, 0, 5)
                for i in range(4):
                    silu(b, 1, i)
                for c in range(NC - 1):
                    copy_T(b, c, 0), copy_T(b, c, 1), silu(b, c + 1, 4), copy_T(b, c, 2), silu(b, c + 1, 5)
                    copy_T(b, c, 3), copy_T(b, c, 4), copy_T(b, c, 5)
                    if c < NC - 2:
                        for i in range(4):
                            silu(b, c + 2, i)
                if with_m:
                    M(b - 1)
                for i in range(6):
                    copy_T(b, NC - 1, i)
                if with_f1:
                    input_T("f1", b + 1)

            def M(b):
                act.wait_ge(m_tr, b + 1)
                act.activation(xT[:, :], bank[0][:, :], ACT.Identity, scale=ln2w, bias=ln2b).then_inc(m_xT, 1)
                for o in range(KB):
                    act.wait_ge(m_up, b * KB + o + 1)
                    act.activation(hid[0][:, o, :], bank[o][:, :], ACT.Gelu, bias=b1[:, o:o + 1]).then_inc(m_gelu, 1)

            def S(b, with_next):
                if with_next:
                    N_logs(b + 1)
                for c in range(NC):
                    for g in range(2):
                        u = slice(H * c + 4 * g, H * c + 4 * g + 4)
                        act.wait_ge(s_w, b * 8 + 2 * c + g + 1)
                        act.activation(V[:, u, :], heads(bank[4 + g]), ACT.Copy).then_inc(s_wc, 1)
                    if with_next and c > 0:
                        decays(b + 1, 2 * c - 2), decays(b + 1, 2 * c - 1)
                    for g in range(2):
                        if with_next and c == NC - 1:
                            silu(b + 1, 0, 2 * g), silu(b + 1, 0, 2 * g + 1)
                        act.wait_ge(s_o, b * 8 + 2 * c + g + 1)
                        act.activation(oT[:, 4 * g:4 * g + 4, :], heads(bank[g]), ACT.Copy).then_inc(s_oc, 1)
                if with_next:
                    decays(b + 1, 6), decays(b + 1, 7), exps(b + 1)

            act.wait_ge(ld_w, 8 * 16)
            input_T("f1", 0), F1(0), N_T(0), N_logs(0)
            for q in range(8):
                decays(0, q)
            exps(0)
            for i in range(4):
                silu(0, 0, i)
            P(0, False, True), F1(1)
            for n in range(1, NJ, 2):
                joined(0, n)
            N_T(1), S(0, True)
            with act.Fori(1, B - 1) as t:
                P(t, True, True), F1(t + 1), input_T("f2", t - 1), F2(t - 1, True, True), S(t, True)
            P(B - 1, True, False), input_T("f2", B - 2), F2(B - 2, True, False), S(B - 1, False)
            M(B - 1), input_T("f2", B - 1), F2(B - 1, False, False)

        @block.tensor
        def _(pe):
            def transposes(rows, done):
                for c in range(NC):
                    last = pe.transpose(bank[0][:, 128 * c:128 * c + 128], rows[:, c, :], ident[:, :])
                last.then_inc(done, 1)

            def half_layer(w, src, k, pair, bk, done):
                for i in range(2):
                    o = 2 * pair + i
                    last = pe.matmul(bank[bk + i][:, :], w[:, k, 128 * o:128 * o + 128], src[:, k, :],
                                     start=(k == 0), stop=(k == KB - 1))
                    if k == KB - 1:
                        last.then_inc(done, 1)

            def down(w, src, k, done):
                for c in range(NC):
                    last = pe.matmul(bank[4][:, 128 * c:128 * c + 128], src[:, k, 128 * c:128 * c + 128], w[:, k, :],
                                     start=(k == 0 and c == 0), stop=(k == KB - 1), skip_group_check=True)
                if k == KB - 1:
                    last.then_inc(done, 1)

            def input_T(n, b):
                pe.wait_ge(ln_f[n].rows, b + 1)
                transposes(xn if n == "f2" else xin, F[n]["tr"])

            def layer1(n, b):
                f = F[n]
                pe.wait_ge(f["xT"], b + 1)
                for o in range(KB):
                    if o >= 2:
                        pe.wait_ge(f["hid"], b * KB + o - 1)
                    for w, bk in ((w1, 2 * (o % 2)), (w2, 2 * (o % 2) + 1)):
                        pe.matmul(bank[bk][:, :], w[:, 128 * o:128 * o + 128], xT[:, :], start=True, stop=True
                                  ).then_inc(f["gate"], 1)

            def slot(n, b, s):
                f, part, k = F[n], s // KB, s % KB
                if part == 0:
                    pe.wait_ge(f["hid"], b * KB + k + 1)
                    half_layer(h1, hid[0], k, 0, 4, f["l2"])
                elif part == 1:
                    half_layer(h1, hid[0], k, 1, 0, f["l2"])
                elif part == 2:
                    pe.wait_ge(f["g2"], b * KB + (2 if k == 0 else k + 1))
                    half_layer(h2, hid[1], k, 0, 4, f["l3"])
                elif part == 3:
                    half_layer(h2, hid[1], k, 1, 2, f["l3"])
                else:
                    pe.wait_ge(f["g3"], b * KB + k + 1)
                    down(w3, hid[0], k, f["l4"])

            def F1(b, with_f2):
                layer1("f1", b)
                for s in range(FFN_SLOTS):
                    if s == 4 * KB and with_f2:
                        input_T("f2", b - 2)
                    if s == 0:
                        if not isinstance(b, int):
                            pe.wait_ge(m_x2, b - 1)
                        if not isinstance(b, int) or b > 0:
                            pe.wait_ge(p_trc, b * 6 * NC)
                    slot("f1", b, s)

            def F2(b, with_join, with_n):
                layer1("f2", b)
                for s in range(FFN_SLOTS):
                    if s == 0 and not isinstance(b, int):
                        pe.wait_ge(F["f1"]["sc"], b + 3)
                    slot("f2", b, s)
                    if with_join and s >= FFN_SLOTS - NJ:
                        join(b + 1, s - (FFN_SLOTS - NJ))
                    if s == 4 * KB - 1 and with_n:
                        N_T(b + 2)

            def N_T(b):
                pe.wait_ge(ln_n1.rows, b + 1)
                transposes(xn1, n_tr)

            def N_logits(b):
                pe.wait_ge(n_nT, b + 1)
                for c in range(NC):
                    last = pe.matmul(bank[2][:, 16 * c:16 * c + 16], nT[:, 128 * c:128 * c + 128], wba[:, :],
                                     start=True, stop=True)
                last.then_inc(n_logit, 1)

            def N_sums(b):
                pe.wait_ge(n_lo, b + 1)
                pe.matmul(bank[2][:, 2 * U:3 * U], triu[:, :], lga[:, :], start=True, stop=True)
                pe.matmul(bank[2][:, 3 * U:4 * U], ones[:, :].to_broadcast([128, 128]), lga[:, :], start=True, stop=True
                          ).then_inc(n_g, 1)

            def decay(b, q):
                if q >= 2:
                    pe.wait_ge(d_exp, b * 8 + q - 1)
                bk = bank[2 + q % 2]
                pe.matmul(bk[:, :], identb[:, :], maskb[:, :].unsqueeze(1).to_broadcast([128, 4, 128]),
                          start=True, stop=False, skip_group_check=True)
                for h in range(4):
                    u = 4 * q + h
                    for part in (lah, lal):
                        last = pe.matmul(heads(bk)[:, h, :], part[:, u:u + 1].to_broadcast([128, 128]), triur[:, :],
                                         start=False, stop=(part is lal and h == 3), skip_group_check=True)
                last.then_inc(d_sum, 1)

            def proj(b, c, i):
                n = 6 * c + i
                if 2 <= n < 4:
                    pe.wait_ge(p_silu, b * 6 * NC + n - 1)
                if n >= 8:
                    pe.wait_ge(p_silu, b * 6 * NC + n - 3)
                bk = bank[6 + n % 2] if n < 4 else bank[n % 4]
                pe.matmul(bk[:, :], nT[:, 128 * c:128 * c + 128], wqkv[:, i // 2, 512 * (i % 2):512 * (i % 2) + 512],
                          start=True, stop=True).then_inc(p_proj, 1)

            def turn(b, c, i):
                n = 6 * c + i
                if i == 0:
                    pe.wait_ge(p_unit, b * NC + c + 1)
                if i == 4:
                    pe.wait_ge(p_qe, b * NC + c + 1)
                if n >= 2:
                    pe.wait_ge(p_trc, b * 6 * NC + n - 1)
                for h in range(4):
                    hh = 4 * (i % 2) + h
                    src = (qk[c % 2][:, 1, hh, :], qk[c % 2][:, 0, hh, :], qe[:, hh, :])[i // 2]
                    last = pe.transpose(bank[4 + n % 2][:, 128 * h:128 * h + 128], src, ident[:, :])
                last.then_inc(p_tr, 1)

            def products(b, c, g, s):
                k = 4 * c + 2 * g + s
                if k < 2:
                    pe.wait_ge(p_silu, b * 6 * NC + 4)
                else:
                    pe.wait_ge(p_am, b * 16 + k - 1)
                pe.wait_ge(p_trc, b * 6 * NC + 6 * c + 1 + g + 2 * s)
                for h in range(4):
                    u = H * c + 4 * g + h
                    last = pe.matmul(heads(bank[6 + s])[:, h, :], KT[:, u, :], (KT[:, u, :], qT[:, 4 * g + h, :])[s],
                                     start=True, stop=True)
                last.then_inc(p_kq, 1)

            def P(b, with_m, with_f1):
                if isinstance(b, int) and b == 0:
                    pe.wait_ge(F["f1"]["sc"], 1)
                else:
                    pe.wait_ge(s_oc, b * 8)
                    pe.wait_ge(s_xa, b * NC)
                pe.wait_ge(d_exp, b * 8 + 8)
                proj(b, 0, 4), proj(b, 0, 5)
                for i in range(4):
                    proj(b, 1, i)
                for c in range(NC):
                    if c == NC - 1 and with_m:
                        M_up(b - 1)
                    turn(b, c, 0), turn(b, c, 1)
                    if c < NC - 1:
                        proj(b, c + 1, 4)
                    turn(b, c, 2)
                    if c < NC - 1:
                        proj(b, c + 1, 5)
                    turn(b, c, 3)
                    products(b, c, 0, 0), turn(b, c, 4), products(b, c, 0, 1)
                    turn(b, c, 5), products(b, c, 1, 0), products(b, c, 1, 1)
                    if c < NC - 2:
                        for i in range(4):
                            proj(b, c + 2, i)
                if with_f1:
                    if with_m:
                        pe.wait_ge(m_gelu, (b - 1) * KB + KB)
                    else:
                        pe.wait_ge(p_silu, b * 6 * NC + 6 * NC)
                    input_T("f1", b + 1)
                if with_m:
                    pe.wait_ge(p_trc, b * 6 * NC + 6 * NC)
                    M_down(b - 1)

            def M_up(b):
                pe.wait_ge(ln_m.rows, b + 1)
                if isinstance(b, int) and b == B - 1:
                    pe.wait_ge(s_oc, B * 8)
                else:
                    pe.wait_ge(p_silu, b * 6 * NC + 12 * NC)
                transposes(xa, m_tr)
                pe.wait_ge(m_xT, b + 1)
                for o in range(KB):
                    pe.matmul(bank[o][:, :], wm1[:, 128 * o:128 * o + 128], xT[:, :], start=True, stop=True
                              ).then_inc(m_up, 1)

            def M_down(b):
                for k in range(KB):
                    pe.wait_ge(m_gelu, b * KB + k + 1)
                    down(wm2, hid[0], k, m_down)

            def hold(bk):
                pe.matmul(bk[:, 0:1], ident[:, :], ident[:, 0:1], start=True, stop=True)

            def join(b, n):
                if n == 0:
                    pe.wait_ge(b_load, b * 7 * 16 + 7 * 16)
                if n >= 2:
                    pe.wait_ge((j_dve, j_act)[n % 2], b * (NJ // 2) + n // 2)
                kind, part = JOINS[n]
                bk = bank[6 + n % 2]
                hold(bk)
                if kind in ("p64", "r64"):
                    for i in range(8):
                        u = 8 * part + i
                        col = slice(64 * i, 64 * i + 64)
                        if kind == "p64":
                            last = pe.matmul(bk[64:128, col], R[0:64, u, 64:128], TB[0:64, u, :], start=True, stop=True)
                        else:
                            last = pe.matmul(bk[0:64, col], TB[64:128, u, :], R[64:128, u, 64:128], start=True, stop=True)
                else:
                    pair, half = part
                    e, o = slice(64 * pair, 64 * pair + 32), slice(64 * pair + 32, 64 * pair + 64)
                    for i in range(16):
                        u = 16 * half + i
                        col = slice(32 * i, 32 * i + 32)
                        if kind == "p32":
                            last = pe.matmul(bk[o, col], R[e, u, o], TB[e, u, 0:32], start=True, stop=True)
                        elif kind == "r32":
                            last = pe.matmul(bk[e, col], TB[o, u, 0:32], R[o, u, o], start=True, stop=True)
                        else:
                            last = pe.matmul(bk[o, col], R[o, u, o], TB[o, u, 0:32], start=True, stop=True)
                last.then_inc(j_full, 1)

            def S(b, with_next):
                if isinstance(b, int) and b == 0:
                    pe.wait_ge(F["f1"]["sc"], 2)
                else:
                    pe.wait_ge(F["f2"]["sc"], b)
                pe.wait_ge(j_dve, b * (NJ // 2) + NJ // 2)
                pe.wait_ge(j_act, b * (NJ // 2) + NJ // 2)
                for c in range(NC):
                    if c > 0:
                        if with_next and c == 1:
                            pe.wait_ge(n_bias, b + 2)
                        if with_next and c > 1:
                            pe.wait_ge(d_exp, (b + 1) * 8 + 2 * c - 2)
                        for g in range(2):
                            pe.wait_ge(s_S, b * 6 + 2 * (c - 1) + g + 1)
                            for h in range(4):
                                u = H * c + 4 * g + h
                                last = pe.matmul(heads(bank[2 + g])[:, h, :], KT[:, u, :], state[:, 4 * g + h, :],
                                                 start=True, stop=True)
                            last.then_inc(s_ks, 1)
                    for g in range(2):
                        if c > 0:
                            pe.wait_ge(s_rhs, b * 6 + 2 * (c - 1) + g + 1)
                            if g == 0:
                                pe.wait_ge(s_xa, b * NC + c)
                        for h in range(4):
                            u = H * c + 4 * g + h
                            last = pe.matmul(heads(bank[4 + g])[:, h, :], R[:, u, :], V[:, u, :], start=True, stop=True)
                        last.then_inc(s_w, 1)
                    if with_next and c > 0:
                        decay(b + 1, 2 * c - 2), decay(b + 1, 2 * c - 1)
                    for g in range(2):
                        if c < NC - 1:
                            pe.wait_ge(s_wc, b * 8 + 2 * c + g + 1)
                            for h in range(4):
                                u = H * c + 4 * g + h
                                last = pe.matmul(heads(bank[6 + g])[:, h, :], KD[:, u, :], V[:, u, :], start=True, stop=True)
                            last.then_inc(s_up, 1)
                        elif with_next:
                            proj(b + 1, 0, 2 * g), proj(b + 1, 0, 2 * g + 1)
                        pe.wait_ge(s_wc, b * 8 + 2 * c + g + 1)
                        for h in range(4):
                            u = H * c + 4 * g + h
                            last = pe.matmul(heads(bank[g])[:, h, :], V[:, u, :], MT[:, u, :], start=True, stop=(c == 0))
                            if c > 0:
                                last = pe.matmul(heads(bank[g])[:, h, :], state[:, 4 * g + h, :], QET[:, u, :],
                                                 start=False, stop=True)
                        last.then_inc(s_o, 1)
                    if with_next and c == 0:
                        N_sums(b + 1)
                    for g in range(2):
                        pe.wait_ge(s_oc, b * 8 + 2 * c + g + 1)
                        for h in range(4):
                            hh = 4 * g + h
                            last = pe.matmul(bank[4][:, 0:D], oT[:, hh, :], wo[:, hh, :], start=(hh == 0), stop=(hh == H - 1))
                    last.then_inc(s_y, 1)
                if with_next:
                    decay(b + 1, 6), decay(b + 1, 7)

            pe.wait_ge(c_pool, 1)
            pe.wait_ge(c_dve, 1)
            pe.wait_ge(ld_w, 8 * 16)
            input_T("f1", 0), F1(0, False)
            pe.wait_ge(ld_a, 8 * 16)
            N_T(0), N_logits(0), N_sums(0)
            pe.wait_ge(n_bias, 1)
            for q in range(8):
                decay(0, q)
            for i in range(4):
                proj(0, 0, i)
            P(0, False, True), F1(1, False)
            for n in range(NJ):
                join(0, n)
            N_T(1), N_logits(1), S(0, True)
            with pe.Fori(1, B - 1) as t:
                P(t, True, True), F1(t + 1, True), F2(t - 1, True, True), N_logits(t + 1), S(t, True)
            P(B - 1, True, False), input_T("f2", B - 2), F2(B - 2, True, False), S(B - 1, False)
            M_up(B - 1)
            pe.wait_ge(s_xa, B * NC)
            M_down(B - 1)
            input_T("f2", B - 1), F2(B - 1, False, False)


def kernel(**inputs):
    import numpy as np
    import concourse.bacc as bacc
    from concourse.bass_utils import run_bass_kernel_spmd

    a = {k: np.asarray(v) for k, v in inputs.items()}
    at, ff = "L0_attn_", "L0_ffn_"

    def column_blocks(v):
        return v.reshape(KB, 128).T

    cols = [column_blocks(a[ff + k]) for k in ("w1_s", "w2_s", "h1_s", "h2_s")] + [column_blocks(a[at + "b1"])]
    cols += [a[at + k].reshape(128, 1) for k in ("ln1_w", "ln1_b", "ln2_w", "ln2_b")]
    host = {
        "x": a[at + "x"], "w1T": a[ff + "w1_w"].T, "w2T": a[ff + "w2_w"].T, "h1T": a[ff + "h1_w"].T,
        "h2T": a[ff + "h2_w"].T, "w3T": a[ff + "w3_w"].T, "s3": a[ff + "w3_s"], "b2": a[at + "b2"],
        "cols": np.concatenate(cols, axis=1),
    }
    host.update({k: a[at + k] for k in ("Wq", "Wk", "Wv", "Wb", "Wa", "Wo", "W1", "W2")})

    nc = bacc.Bacc("TRN2", target_bir_lowering=False, num_devices=1)
    arrays, aps = {}, {}
    for name, v in host.items():
        arrays["in_" + name] = np.ascontiguousarray(v)
        aps[name] = nc.dram_tensor("in_" + name, v.shape, mybir.dt.from_np(v.dtype), kind="ExternalInput").ap()
    aps["out"] = nc.dram_tensor("out_x", (B, T, D), mybir.dt.float32, kind="ExternalOutput").ap()
    build_program(nc, aps)
    r = run_bass_kernel_spmd(nc, [arrays], core_ids=[0])
    return r.results[0]["out_x"]
```

```python
from contextlib import ExitStack

import concourse.bass as bass
from concourse import mybir

B, T, D, H, HID = 8, 512, 128, 8, 512
C = 128
NC = T // C
U = NC * H
KB = HID // 128
BS = 32
NBLK = C // BS
EPS_LN, EPS_L2 = 1e-5, 1e-6
NEG = -1e30
RSQRT_STEPS = 11
ALL = range(KB)
FFN_SLOTS = 5 * KB


def build_program(nc, d):
    f32, f32r, bf16, i32 = mybir.dt.float32, mybir.dt.float32r, mybir.dt.bfloat16, mybir.dt.int32
    ALU, ACT, AX = mybir.AluOpType, mybir.ActivationFunctionType, mybir.AxisListType
    ctx = ExitStack()
    with ctx:
        def sb(name, shape, dt=f32):
            return ctx.enter_context(nc.sbuf_tensor(name, shape, dt))

        def sem(name):
            return ctx.enter_context(nc.semaphore(name))

        w1 = sb("w1", [128, HID])
        w2 = sb("w2", [128, HID])
        h1 = sb("h1", [128, KB, HID])
        h2 = sb("h2", [128, KB, HID])
        w3 = sb("w3", [128, KB, D])
        wqkv = sb("wqkv", [128, 3, H * 128])
        wba = sb("wba", [128, 2 * H])
        wo = sb("wo", [128, H, D])
        wm1 = sb("wm1", [128, HID])
        wm2 = sb("wm2", [128, KB, D])
        cols = sb("cols", [128, 24])
        s1, s2, sh1, sh2, b1 = (cols[:, 4 * i:4 * i + 4] for i in range(5))
        ln1w, ln1b, ln2w, ln2b = (cols[:, 20 + i:21 + i] for i in range(4))
        s3row = sb("s3row", [128, D])
        b2row = sb("b2row", [128, D])

        ident = sb("ident", [128, 128])
        identb = sb("identb", [128, 128], bf16)
        triu = sb("triu", [128, 128])
        triur = sb("triur", [128, 128], f32r)
        ones = sb("ones", [128, 1])
        maskb = sb("maskb", [128, 128], bf16)

        xin = sb("xin", [128, NC, D])
        x1 = sb("x1", [128, NC, D])
        x1m = sb("x1m", [128, NC, D])
        x2 = sb("x2", [128, NC, D])
        n0 = sb("n0", [128, NC, D])
        xa = sb("xa", [128, NC, D])
        rows_or_qe = sb("rows_or_qe", [128, 2 * T])
        xn = rows_or_qe[:, 0:T].rearrange("p (c n) -> p c n", c=NC)
        xn1 = rows_or_qe[:, T:].rearrange("p (c n) -> p c n", c=NC)
        qe = rows_or_qe[:, :].rearrange("p (h n) -> p h n", h=H)
        xT = sb("xT", [128, T])
        nT = sb("nT", [128, T])

        big = [sb("big0", [128, 2 * H * 128]), sb("big1", [128, 2 * H * 128])]
        hid = [t[:, :].rearrange("p (k n) -> p k n", k=KB) for t in big]
        own, other = {"f1": hid[1], "f2": hid[0]}, {"f1": hid[0], "f2": hid[1]}
        qk = [t[:, :].rearrange("p (s h n) -> p s h n", s=2, h=H) for t in big]
        mid = sb("mid", [128, H * 128])
        sg = mid[:, :].rearrange("p (s n) -> p s n", s=2)
        qT = mid[:, :].rearrange("p (h n) -> p h n", h=H)
        oT = qT

        V = sb("V", [128, U, 128])
        KD = sb("KD", [128, U, 128])
        KT = sb("KT", [128, U, 128])
        QET = sb("QET", [128, U, 128])
        R = sb("R", [128, U, 128])
        MT = sb("MT", [128, U, 128])
        TB = sb("TB", [128, U, 64])
        state = sb("state", [128, H, 128])
        blkA = sb("blkA", [128, BS * BS])
        blkT = sb("blkT", [128, BS * BS])
        blkP = sb("blkP", [128, 256])

        absz = sb("absz", [128, NC * 2 * H])
        ez = sb("ez", [128, NC * 2 * H])
        lz = sb("lz", [128, NC * 2 * H])
        lgb = sb("lgb", [128, U])
        lga = sb("lga", [128, U])
        lah = sb("lah", [128, U], f32r)
        lal = sb("lal", [128, U], f32r)
        gn = sb("gn", [128, 2 * U])
        biasj = sb("biasj", [128, U])
        kdl = sb("kdl", [128, U])
        kds = sb("kds", [128, U])
        eg = sb("eg", [128, U])
        egn = sb("egn", [128, U])
        egC = sb("egC", [128, U])
        bst = sb("bst", [128, 2 * H, 6])
        bsq = sb("bsq", [128, 2 * H, 2])
        bss = sb("bss", [128, 2 * H, 2])
        ssq = sb("ssq", [128, 2 * H])
        rnorm = sb("rnorm", [128, 2 * H])
        mhalf = sb("mhalf", [128, 1])

        bank = [ctx.enter_context(nc.psum_tensor(f"bank{i}", [128, 512], f32)) for i in range(8)]

        def heads(bk):
            return bk[:, :].rearrange("p (h n) -> p h n", h=4)

        blocks_out = nc.dram_tensor("blocks_out", [NBLK, U, BS, BS], f32).ap()
        t_back = nc.dram_tensor("t_back", [NBLK, U, BS, BS], f32).ap()
        r_back = nc.dram_tensor("r_back", [NBLK, U, BS, BS], f32).ap()

        ld_x = sem("ld_x")
        ld_w = sem("ld_w")
        ld_h = sem("ld_h")
        ld_a = sem("ld_a")
        c_mem = sem("c_mem")
        c_pool = sem("c_pool")
        c_dve = sem("c_dve")
        st_out = sem("st_out")

        class Site:
            def __init__(self, n, steps=1):
                self.steps = steps
                self.stats, self.aggr, self.var = sem(n + "_stats"), sem(n + "_aggr"), sem(n + "_var")
                self.sq, self.newton, self.rows = sem(n + "_sq"), sem(n + "_newton"), sem(n + "_rows")
                self.st, self.mean = sb(n + "_st", [128, NC, 6]), sb(n + "_mean", [128, NC])
                self.ve, self.rs = sb(n + "_ve", [128, NC]), sb(n + "_rs", [128, NC])
                self.ta, self.tb = sb(n + "_ta", [128, NC]), sb(n + "_tb", [128, NC])

        ln_f = {"f1": Site("lnf1", RSQRT_STEPS), "f2": Site("lnf2", RSQRT_STEPS)}
        ln_m, ln_n0, ln_n1 = Site("lnm"), Site("lnn0"), Site("lnn1")

        def ffn_sems(n):
            names = ("tr", "xT", "gate", "silu", "hid", "l2", "g2", "l3", "g3", "l4", "sc", "res")
            return {k: sem(f"{n}_{k}") for k in names}

        F = {"f1": ffn_sems("f1"), "f2": ffn_sems("f2")}
        ld_x1 = sem("ld_x1")
        x1_moved = sem("x1_moved")
        n_tr, n_nT, n_logit = sem("n_tr"), sem("n_nT"), sem("n_logit")
        n_abs, n_exp, n_ln, n_lg = (sem("n_" + k) for k in ("abs", "exp", "ln", "lg"))
        n_hi, n_lo, n_g, n_gn, n_bias = (sem("n_" + k) for k in ("hi", "lo", "g", "gn", "bias"))
        p_gexp, p_kdl, p_kds, p_egn = (sem("p_" + k) for k in ("gexp", "kdl", "kds", "egn"))
        d_sum, d_exp = sem("d_sum"), sem("d_exp")
        p_proj, p_silu = sem("p_proj"), sem("p_silu")
        p_bst, p_ss1, p_ss2, p_ssq = (sem("p_" + k) for k in ("bst", "ss1", "ss2", "ssq"))
        p_norm = sem("p_norm")
        p_unit, p_kd, p_qe = sem("p_unit"), sem("p_kd"), sem("p_qe")
        p_tr, p_trc = sem("p_tr"), sem("p_trc")
        p_kq, p_am = sem("p_kq"), sem("p_am")
        b_out, b_in = sem("b_out"), sem("b_in")
        b_init, b_prod, b_R = sem("b_init"), sem("b_prod"), sem("b_R")
        b_Tout, b_Rout = sem("b_Tout"), sem("b_Rout")
        b_TB, b_Rin = sem("b_TB"), sem("b_Rin")
        j_full, j_dve, j_act = sem("j_full"), sem("j_dve"), sem("j_act")
        s_ks, s_rhs = sem("s_ks"), sem("s_rhs")
        s_w, s_wc = sem("s_w"), sem("s_wc")
        s_up, s_S = sem("s_up"), sem("s_S")
        s_o, s_oc = sem("s_o"), sem("s_oc")
        s_y, s_xa = sem("s_y"), sem("s_xa")
        m_tr, m_xT, m_up, m_gelu, m_down = (sem("m_" + k) for k in ("tr", "xT", "up", "gelu", "down"))
        m_xab, m_xab2, m_x2 = sem("m_xab"), sem("m_xab2"), sem("m_x2")

        JOINS = [("p32", (0, 0)), ("p32", (1, 0)), ("p32", (0, 1)), ("p32", (1, 1)),
                 ("r32", (0, 0)), ("t32", (0, 0)), ("r32", (0, 1)), ("t32", (0, 1)), ("r32", (1, 0)), ("r32", (1, 1)),
                 ("p64", 0), ("p64", 1), ("p64", 2), ("p64", 3), ("r64", 0), ("r64", 1), ("r64", 2), ("r64", 3)]
        NJ = len(JOINS)

        def join_result(n):
            kind, part = JOINS[n]
            bk = bank[6 + n % 2]
            if kind in ("p64", "r64"):
                u = slice(8 * part, 8 * part + 8)
                src = bk[:, :].rearrange("p (u n) -> p u n", u=8)
                return (src[64:128], TB[64:128, u, :], -1.0) if kind == "p64" else (src[0:64], R[0:64, u, 64:128], 1.0)
            pair, half = part
            u = slice(16 * half, 16 * half + 16)
            e, o = slice(64 * pair, 64 * pair + 32), slice(64 * pair + 32, 64 * pair + 64)
            src = bk[:, :].rearrange("p (u n) -> p u n", u=16)
            if kind == "p32":
                return src[o], TB[o, u, 0:32], -1.0
            return (src[o], TB[o, u, 0:32], 1.0) if kind == "t32" else (src[e], R[e, u, o], 1.0)

        block = ctx.enter_context(nc.Block())

        @block.sync
        def _(sp):
            def rows_of(x, b):
                return x[bass.ds(b, 1), :, :].rearrange("o (c p) n -> p (o c) n", p=128)

            def load_xin(b):
                if not isinstance(b, int) or b > 0:
                    sp.wait_ge(F["f1"]["tr"], b)
                sp.dma_start(xin[:, :, :], rows_of(d["x"], b)).then_inc(ld_x, 16)

            def load_x1(b):
                if not isinstance(b, int) or b > 0:
                    sp.wait_ge(x1_moved, b)
                sp.dma_start(x1[:, :, :], rows_of(d["x"], b)).then_inc(ld_x1, 16)

            load_xin(0)
            for dst, src in ((cols[:, :], d["cols"]), (w1[:, :], d["w1T"]), (w2[:, :], d["w2T"])):
                sp.dma_start(dst, src).then_inc(ld_w, 16)
            for dst, src in ((h1[:, :, :], d["h1T"].rearrange("(k p) n -> p k n", p=128)),
                             (h2[:, :, :], d["h2T"].rearrange("(k p) n -> p k n", p=128)),
                             (w3[:, :, :], d["w3T"].rearrange("(k p) n -> p k n", p=128)),
                             (s3row[:, :], d["s3"].partition_broadcast(128)),
                             (b2row[:, :], d["b2"].partition_broadcast(128))):
                sp.dma_start(dst, src).then_inc(ld_h, 16)
            load_x1(0)
            for dst, src in ((wba[:, 0:H], d["Wb"]), (wba[:, H:], d["Wa"]),
                             (wqkv[:, 0, :], d["Wq"]), (wqkv[:, 1, :], d["Wk"]), (wqkv[:, 2, :], d["Wv"]),
                             (wo[:, :, :], d["Wo"].rearrange("(h p) n -> p h n", p=128)),
                             (wm1[:, :], d["W1"]),
                             (wm2[:, :, :], d["W2"].rearrange("(k p) n -> p k n", p=128))):
                sp.dma_start(dst, src).then_inc(ld_a, 16)

            def P(b):
                for c in range(NC):
                    sp.wait_ge(p_am, b * 16 + 4 * c + 3)
                    for p in range(NBLK):
                        r = slice(BS * p, BS * p + BS)
                        sp.dma_start(blocks_out[p, H * c:H * c + H, :, :].rearrange("u j i -> j u i"),
                                     R[r, H * c:H * c + H, r]).then_inc(b_out, 16)
                sp.wait_ge(b_out, b * 256 + 256)
                sp.dma_start(blkA[:, :], blocks_out.rearrange("p u j i -> (p u) (j i)")).then_inc(b_in, 16)

            def back(b):
                sp.wait_ge(b_prod, b * 2 * (BS - 1) + 2 * (BS - 1))
                sp.dma_start(t_back.rearrange("p u i c -> (p u) (i c)"), blkT[:, :]).then_inc(b_Tout, 16)
                sp.wait_ge(b_R, b + 1)
                sp.dma_start(r_back.rearrange("p u c i -> (p u) (c i)"), blkA[:, :]).then_inc(b_Rout, 16)
                sp.wait_ge(b_Tout, b * 16 + 16)
                for p, col in ((0, 0), (2, 0), (1, BS)):
                    sp.dma_start(TB[BS * p:BS * p + BS, :, col:col + BS],
                                 t_back[p, :, :, :].rearrange("u i c -> i u c")).then_inc(b_TB, 16)
                sp.wait_ge(b_Rout, b * 16 + 16)
                for p in range(NBLK):
                    r = slice(BS * p, BS * p + BS)
                    sp.dma_start(R[r, :, r], r_back[p, :, :, :].rearrange("u c i -> c u i")).then_inc(b_Rin, 16)

            def store(b):
                sp.wait_ge(F["f2"]["res"], b + 1)
                sp.dma_start(rows_of(d["out"], b), x2[:, :, :]).then_inc(st_out, 16)

            load_xin(1)
            P(0), load_x1(1), load_xin(2), back(0)
            with sp.Fori(1, B - 2) as t:
                P(t), load_x1(t + 1), load_xin(t + 2), back(t), store(t - 1)
            P(B - 2), load_x1(B - 1), back(B - 2), store(B - 3)
            P(B - 1), back(B - 1), store(B - 2), store(B - 1)
            sp.wait_ge(st_out, B * 16)

        @block.gpsimd
        def _(pool):
            pool.memset(ident[:, :], 0.0)
            pool.memset(triu[:, :], 1.0)
            pool.memset(identb[:, :], 0.0)
            pool.memset(maskb[:, :], 0.0).then_inc(c_mem, 1)
            pool.memset(ones[:, :], 1.0)
            pool.memset(mhalf[:, :], -0.5)
            pool.memset(TB[:, :, :], 0.0)
            pool.wait_ge(c_mem, 1)
            pool.affine_select(out=ident[:, :], in_=ident[:, :], compare_op=ALU.not_equal, fill=1.0,
                               base=0, pattern=[[-1, 128]], channel_multiplier=1)
            pool.affine_select(out=identb[:, :], in_=identb[:, :], compare_op=ALU.not_equal, fill=1.0,
                               base=0, pattern=[[-1, 128]], channel_multiplier=1)
            pool.affine_select(out=triu[:, :], in_=triu[:, :], compare_op=ALU.is_ge, fill=0.0,
                               base=0, pattern=[[1, 128]], channel_multiplier=-1)
            pool.affine_select(out=maskb[:, :], in_=maskb[:, :], compare_op=ALU.is_ge, fill=NEG,
                               base=0, pattern=[[1, 128]], channel_multiplier=-1).then_inc(c_pool, 1)

            def norms(b, c):
                pool.wait_ge(p_ssq, b * NC + c + 1)
                pool.tensor_tensor(rnorm[:, :], ssq[:, :], mhalf[:, :].to_broadcast([128, 2 * H]), ALU.pow
                                   ).then_inc(p_norm, 1)

            def scaled(b, c):
                u = slice(H * c, H * c + H)
                pool.wait_ge(p_unit, b * NC + c + 1)
                if c == 0:
                    pool.wait_ge(p_kds, b + 1)
                    pool.wait_ge(p_gexp, b + 1)
                pool.tensor_tensor(KD[:, u, :], qk[c % 2][:, 1, :, :],
                                   kds[:, u].unsqueeze(2).to_broadcast([128, H, 128]), ALU.mult).then_inc(p_kd, 1)
                if c > 0:
                    pool.wait_ge(p_tr, b * 6 * NC + 6 * c)
                pool.tensor_tensor(qe[:, :, :], qk[c % 2][:, 0, :, :],
                                   eg[:, u].unsqueeze(2).to_broadcast([128, H, 128]), ALU.mult).then_inc(p_qe, 1)

            A3 = blkA[:, :].rearrange("q (j i) -> q j i", j=BS)
            T3 = blkT[:, :].rearrange("q (i c) -> q i c", i=BS)

            def invert(b):
                pool.wait_ge(b_init, b * 2 + 2)
                pool.wait_ge(b_in, b * 16 + 16)
                steps = 2 * (BS - 1)
                for j in range(BS - 1):
                    n, m = BS - 1 - j, j + 1
                    prod = blkP[:, 0:n * m].rearrange("q (i c) -> q i c", i=n)
                    if j > 0:
                        pool.wait_ge(b_prod, b * steps + 2 * j)
                    pool.tensor_tensor(prod, A3[:, j, j + 1:].unsqueeze(2).to_broadcast([128, n, m]),
                                       T3[:, j:j + 1, 0:m].to_broadcast([128, n, m]), ALU.mult).then_inc(b_prod, 1)
                    pool.wait_ge(b_prod, b * steps + 2 * j + 1)
                    pool.tensor_tensor(T3[:, j + 1:, 0:m], T3[:, j + 1:, 0:m], prod, ALU.subtract).then_inc(b_prod, 1)
                pool.wait_ge(b_prod, b * steps + steps)
                pool.tensor_tensor(A3, T3.rearrange("q i c -> q c i"),
                                   ones[:, :].unsqueeze(2).to_broadcast([128, BS, BS]), ALU.mult).then_inc(b_R, 1)

            def M(b):
                pool.wait_ge(s_xa, b * NC + NC)
                pool.wait_ge(x1_moved, b + 1)
                pool.tensor_tensor(x1m[:, :, :], xa[:, :, :], x1m[:, :, :], ALU.add).then_inc(m_xab, 1)
                pool.wait_ge(m_xab, b + 1)
                pool.tensor_tensor(x1m[:, :, :], x1m[:, :, :],
                                   b2row[:, :].unsqueeze(1).to_broadcast([128, NC, D]), ALU.add).then_inc(m_xab2, 1)

            def inverse(s, b):
                pool.wait_ge(s.var, b + 1)
                pool.tensor_tensor(s.rs[:, :], s.ve[:, :], mhalf[:, :].to_broadcast([128, NC]), ALU.pow
                                   ).then_inc(s.newton, 1)

            def P(b, with_m):
                norms(b, 0)
                if with_m:
                    M(b - 1)
                scaled(b, 0)
                norms(b, 1), scaled(b, 1)
                if with_m:
                    inverse(ln_m, b - 1)
                for c in range(2, NC):
                    norms(b, c), scaled(b, c)
                invert(b)

            def N(b):
                inverse(ln_n0, b), inverse(ln_n1, b)

            pool.wait_ge(ld_h, 5 * 16)
            N(0), P(0, False), N(1)
            with pool.Fori(1, B - 1) as t:
                P(t, True), N(t + 1)
            P(B - 1, True), M(B - 1), inverse(ln_m, B - 1)

        @block.vector
        def _(dve):

            def rsqrt(done, b, x, y, ta, tb):
                n = b * RSQRT_STEPS
                dve.tensor_scalar(ta.bitcast(i32), x.bitcast(i32), 1, None, ALU.arith_shift_right).then_inc(done, 1)
                dve.wait_ge(done, n + 1)
                dve.tensor_scalar(y.bitcast(i32), ta.bitcast(i32), -1, 0x5F3759DF, ALU.mult, ALU.add).then_inc(done, 1)
                for i in range(3):
                    dve.wait_ge(done, n + 3 * i + 2)
                    dve.tensor_tensor(ta, y, y, ALU.mult).then_inc(done, 1)
                    dve.wait_ge(done, n + 3 * i + 3)
                    dve.scalar_tensor_tensor(out=tb, in0=ta, scalar=-0.5, in1=x, op0=ALU.mult, op1=ALU.mult
                                             ).then_inc(done, 1)
                    dve.wait_ge(done, n + 3 * i + 4)
                    dve.scalar_tensor_tensor(out=y, in0=tb, scalar=1.5, in1=y, op0=ALU.add, op1=ALU.mult
                                             ).then_inc(done, 1)

            def moments(s, b, x):
                for c in range(NC):
                    last = dve.bn_stats(s.st[:, c, :], x[:, c, :])
                last.then_inc(s.stats, 1)
                dve.wait_ge(s.stats, b + 1)
                dve.tensor_tensor(s.mean[:, :], s.st[:, :, 1], s.st[:, :, 4], ALU.add)
                dve.tensor_tensor(s.ta[:, :], s.st[:, :, 1], s.st[:, :, 4], ALU.subtract)
                dve.tensor_tensor(s.tb[:, :], s.st[:, :, 2], s.st[:, :, 5], ALU.add).then_inc(s.aggr, 1)
                dve.wait_ge(s.aggr, b + 1)
                dve.tensor_scalar(s.mean[:, :], s.mean[:, :], 0.5, None, ALU.mult)
                dve.tensor_scalar(s.ve[:, :], s.tb[:, :], 1.0 / D, EPS_LN, ALU.mult, ALU.add)
                dve.scalar_tensor_tensor(out=s.ta[:, :], in0=s.ta[:, :], scalar=0.25, in1=s.ta[:, :],
                                         op0=ALU.mult, op1=ALU.mult).then_inc(s.sq, 1)
                dve.wait_ge(s.sq, b + 1)
                dve.tensor_tensor(s.ve[:, :], s.ve[:, :], s.ta[:, :], ALU.add).then_inc(s.var, 1)

            def normed(s, b, x, out):
                dve.wait_ge(s.newton, b * s.steps + s.steps)
                for c in range(NC):
                    last = dve.tensor_scalar(out[:, c, :], x[:, c, :], s.mean[:, c:c + 1], s.rs[:, c:c + 1],
                                             ALU.subtract, ALU.mult)
                last.then_inc(s.rows, 1)

            def layernorm(s, b, x, out):
                moments(s, b, x)
                if s.steps > 1:
                    dve.wait_ge(s.var, b + 1)
                    rsqrt(s.newton, b, s.ve[:, :], s.rs[:, :], s.ta[:, :], s.tb[:, :])
                normed(s, b, x, out)

            def LN_F1(b):
                dve.wait_ge(ld_x, b * 16 + 16)
                layernorm(ln_f["f1"], b, xin, xin)

            def LN_F2(b):
                dve.wait_ge(m_x2, b + 1)
                layernorm(ln_f["f2"], b, x2, xn)

            def M_moments(b):
                dve.wait_ge(s_xa, b * NC + NC)
                moments(ln_m, b, xa)

            def M_normed(b):
                dve.wait_ge(m_xab, b + 1)
                normed(ln_m, b, xa, xa)

            def gating(n, b, blocks):
                f = F[n]
                for o in blocks:
                    dve.wait_ge(f["gate"], b * 2 * KB + 2 * o + 2)
                    dve.wait_ge(f["silu"], b * KB + o + 1)
                    dve.scalar_tensor_tensor(out=own[n][:, o, :], in0=bank[1 + 2 * (o % 2)][:, :], scalar=s2[:, o:o + 1],
                                             in1=sg[:, o % 2, :], op0=ALU.mult, op1=ALU.mult).then_inc(f["hid"], 1)

            def result(n, b, x):
                f = F[n]
                dve.wait_ge(f["l4"], b + 1)
                dve.tensor_tensor(xn[:, :, :], heads(bank[4]), s3row[:, :].unsqueeze(1).to_broadcast([128, NC, D]),
                                  ALU.mult).then_inc(f["sc"], 1)
                dve.wait_ge(f["sc"], b + 1)
                dve.tensor_tensor(x[:, :, :], xn[:, :, :], x[:, :, :], ALU.add).then_inc(f["res"], 1)

            def F1_result(b):
                dve.wait_ge(ld_x1, b * 16 + 16)
                result("f1", b, x1)

            def N0(b):
                dve.wait_ge(F["f1"]["res"], b + 1)
                layernorm(ln_n0, b, x1, n0)

            def N1(b):
                dve.wait_ge(ln_n0.rows, b + 1)
                layernorm(ln_n1, b, n0, xn1)

            def gates(b):
                dve.wait_ge(n_logit, b + 1)
                z = bank[2][:, 0:NC * 2 * H]
                dve.tensor_scalar(lz[:, :], z, -1.0, None, ALU.mult).then_inc(n_abs, 1)
                dve.wait_ge(n_abs, b * 2 + 1)
                dve.tensor_tensor(absz[:, :], z, lz[:, :], ALU.max).then_inc(n_abs, 1)
                dve.wait_ge(n_ln, b + 1)
                z4 = z.rearrange("p (c s h) -> p c s h", c=NC, s=2)
                l4 = lz[:, :].rearrange("p (c s h) -> p c s h", c=NC, s=2)
                for s, dst in ((0, lgb), (1, lga)):
                    last = dve.scalar_tensor_tensor(out=dst[:, :].rearrange("p (c h) -> p c h", c=NC), in0=z4[:, :, s, :],
                                                    scalar=0.0, in1=l4[:, :, s, :], op0=ALU.min, op1=ALU.subtract)
                last.then_inc(n_lg, 1)
                dve.wait_ge(n_lg, b + 1)
                dve.tensor_copy(lah[:, :], lga[:, :]).then_inc(n_hi, 1)
                dve.wait_ge(n_hi, b + 1)
                dve.tensor_tensor(lal[:, :], lga[:, :], lah[:, :].bitcast(f32), ALU.subtract).then_inc(n_lo, 1)

            def cumulated(b):
                dve.wait_ge(n_g, b + 1)
                dve.tensor_copy(gn[:, :], bank[2][:, 2 * U:4 * U]).then_inc(n_gn, 1)
                dve.tensor_tensor(biasj[:, :], lgb[:, :], bank[2][:, 2 * U:3 * U], ALU.subtract).then_inc(n_bias, 1)

            def vectors(b):
                if not isinstance(b, int) or b > 0:
                    dve.wait_ge(b_Tout, b * 16)
                dve.memset(blkT[:, :], 0.0).then_inc(b_init, 1)
                dve.wait_ge(b_init, b * 2 + 1)
                dve.memset(blkT[:, 0:BS * BS:BS + 1], 1.0).then_inc(b_init, 1)
                dve.wait_ge(n_bias, b + 1)
                dve.tensor_tensor(kdl[:, :], biasj[:, :], gn[:, U:2 * U], ALU.add).then_inc(p_kdl, 1)
                dve.wait_ge(p_gexp, b + 1)
                dve.tensor_scalar(egn[:, :], eg[:, :], -1.0, None, ALU.mult).then_inc(p_egn, 1)

            def squares(b, c):
                dve.wait_ge(p_silu, b * 6 * NC + 6 * c + 4)
                for i in range(2 * H):
                    last = dve.bn_stats(bst[:, i, :], qk[c % 2][:, i // H, i % H, :])
                last.then_inc(p_bst, 1)
                k = b * NC + c
                dve.wait_ge(p_bst, k + 1)
                dve.tensor_tensor(bsq[:, :, :], bst[:, :, 1::3], bst[:, :, 1::3], ALU.mult).then_inc(p_ss1, 1)
                dve.wait_ge(p_ss1, k + 1)
                dve.scalar_tensor_tensor(out=bss[:, :, :], in0=bsq[:, :, :], scalar=64.0, in1=bst[:, :, 2::3],
                                         op0=ALU.mult, op1=ALU.add).then_inc(p_ss2, 1)
                dve.wait_ge(p_ss2, k + 1)
                dve.scalar_tensor_tensor(out=ssq[:, :], in0=bss[:, :, 0], scalar=EPS_L2, in1=bss[:, :, 1],
                                         op0=ALU.add, op1=ALU.add).then_inc(p_ssq, 1)

            def unit(b, c):
                dve.wait_ge(p_norm, b * NC + c + 1)
                flat = qk[c % 2].rearrange("p s h n -> p (s h) n")
                dve.tensor_tensor(flat, flat, rnorm[:, :].unsqueeze(2).to_broadcast([128, 2 * H, 128]), ALU.mult
                                  ).then_inc(p_unit, 1)

            def decayed(b, c):
                dve.wait_ge(d_exp, b * 8 + 2 * c + 2)
                for g in range(2):
                    u = slice(H * c + 4 * g, H * c + 4 * g + 4)
                    dve.wait_ge(p_kq, b * 16 + 4 * c + 2 * g + 1)
                    dve.tensor_tensor(R[:, u, :], heads(bank[6]), MT[:, u, :], ALU.mult).then_inc(p_am, 1)
                    dve.wait_ge(p_kq, b * 16 + 4 * c + 2 * g + 2)
                    dve.tensor_tensor(MT[:, u, :], heads(bank[7]), MT[:, u, :], ALU.mult).then_inc(p_am, 1)

            def P(b, with_m, with_f1):
                for c in range(1, NC):
                    squares(b, c), decayed(b, c - 1), unit(b, c)
                    if c == 1 and with_m:
                        M_moments(b - 1)
                    if c == 2 and with_m:
                        M_normed(b - 1)
                if with_f1:
                    LN_F1(b + 1)
                decayed(b, NC - 1)

            def M_result(b):
                dve.wait_ge(m_xab2, b + 1)
                if not isinstance(b, int) or b > 0:
                    dve.wait_ge(st_out, b * 16)
                dve.wait_ge(m_down, b + 1)
                dve.tensor_tensor(x2[:, :, :], heads(bank[4]), x1m[:, :, :], ALU.add).then_inc(m_x2, 1)

            def move(b):
                if not isinstance(b, int) or b > 0:
                    dve.wait_ge(m_x2, b)
                dve.tensor_copy(xa[:, :, :], n0[:, :, :])
                dve.tensor_copy(x1m[:, :, :], x1[:, :, :]).then_inc(x1_moved, 1)

            def joined(b, n):
                src, dst, factor = join_result(n)
                dve.wait_ge(j_full, b * NJ + n + 1)
                dve.tensor_scalar(dst, src, factor, None, ALU.mult).then_inc(j_dve, 1)

            def J(b, first):
                for n in range(first, NJ, 2):
                    joined(b, n)

            def S(b, with_next):
                if with_next:
                    gates(b + 1)
                for c in range(NC):
                    if c == 1:
                        dve.wait_ge(p_egn, b + 1)
                    if c > 0:
                        for g in range(2):
                            dve.wait_ge(s_ks, b * 6 + 2 * (c - 1) + g + 1)
                            for h in range(4):
                                u = H * c + 4 * g + h
                                last = dve.scalar_tensor_tensor(out=V[:, u, :], in0=heads(bank[2 + g])[:, h, :],
                                                                scalar=egn[:, u:u + 1], in1=V[:, u, :],
                                                                op0=ALU.mult, op1=ALU.add)
                            last.then_inc(s_rhs, 1)
                    if c < NC - 1:
                        for g in range(2):
                            dve.wait_ge(s_up, b * 6 + 2 * c + g + 1)
                            if c == 0:
                                dve.tensor_copy(state[:, 4 * g:4 * g + 4, :], heads(bank[6 + g])).then_inc(s_S, 1)
                            else:
                                for h in range(4):
                                    hh = 4 * g + h
                                    last = dve.scalar_tensor_tensor(out=state[:, hh, :], in0=state[:, hh, :],
                                                                    scalar=egC[:, H * c + hh:H * c + hh + 1],
                                                                    in1=heads(bank[6 + g])[:, h, :],
                                                                    op0=ALU.mult, op1=ALU.add)
                                last.then_inc(s_S, 1)
                    elif with_next:
                        squares(b + 1, 0)
                    if with_next and c == 0:
                        cumulated(b + 1)
                    dve.wait_ge(s_y, b * NC + c + 1)
                    if c == 0:
                        dve.wait_ge(x1_moved, b + 1)
                    dve.tensor_tensor(xa[:, c, :], bank[4][:, 0:D], xa[:, c, :], ALU.add).then_inc(s_xa, 1)
                if with_next:
                    vectors(b + 1), unit(b + 1, 0)

            LN_F1(0)
            dve.wait_ge(c_pool, 1)
            dve.tensor_copy(triur[:, :], triu[:, :]).then_inc(c_dve, 1)
            dve.wait_ge(ld_w, 3 * 16)
            gating("f1", 0, ALL)
            dve.wait_ge(ld_h, 5 * 16)
            dve.tensor_scalar(s3row[:, :], s3row[:, :], 0.5, None, ALU.mult).then_inc(c_dve, 1)
            dve.wait_ge(c_dve, 2)
            F1_result(0), N0(0), N1(0), gates(0), squares(0, 0), cumulated(0)
            unit(0, 0), vectors(0), P(0, False, True), move(0)
            gating("f1", 1, ALL), F1_result(1), N0(1), N1(1), J(0, 0), S(0, True)
            with dve.Fori(1, B - 1) as t:
                P(t, True, True)
                gating("f1", t + 1, (0, 1)), M_result(t - 1), gating("f1", t + 1, (2, 3)), move(t), LN_F2(t - 1)
                gating("f2", t - 1, (0, 1)), F1_result(t + 1), gating("f2", t - 1, (2, 3))
                N0(t + 1), joined(t, 0)
                dve.wait_ge(ln_n0.rows, t + 2)
                moments(ln_n1, t + 1, n0), joined(t, 2), normed(ln_n1, t + 1, n0, xn1), J(t, 4)
                result("f2", t - 1, x2), S(t, True)
            P(B - 1, True, False), M_result(B - 2), move(B - 1), LN_F2(B - 2)
            gating("f2", B - 2, ALL), result("f2", B - 2, x2), J(B - 1, 0), S(B - 1, False)
            M_moments(B - 1), M_normed(B - 1), M_result(B - 1), LN_F2(B - 1), gating("f2", B - 1, ALL), result("f2", B - 1, x2)

        @block.scalar
        def _(act):
            def input_T(n, b):
                act.wait_ge(F[n]["tr"], b + 1)
                act.activation(xT[:, :], bank[0][:, :], ACT.Copy).then_inc(F[n]["xT"], 1)

            def silus_F(n, b):
                f = F[n]
                for o in range(KB):
                    act.wait_ge(f["gate"], b * 2 * KB + 2 * o + 1)
                    if o >= 2:
                        act.wait_ge(f["hid"], b * KB + o - 1)
                    act.activation(sg[:, o % 2, :], bank[2 * (o % 2)][:, :], ACT.Silu, scale=s1[:, o:o + 1]
                                   ).then_inc(f["silu"], 1)

            def gelus2(n, b, pair):
                for i in range(2):
                    o = 2 * pair + i
                    act.wait_ge(F[n]["l2"], b * KB + o + 1)
                    act.activation(other[n][:, o, :], bank[(4, 0)[pair] + i][:, :], ACT.Gelu, scale=sh1[:, o:o + 1]
                                   ).then_inc(F[n]["g2"], 1)

            def gelus3(n, b, pair):
                for i in range(2):
                    o = 2 * pair + i
                    act.wait_ge(F[n]["l3"], b * KB + o + 1)
                    act.activation(own[n][:, o, :], bank[(4, 2)[pair] + i][:, :], ACT.Gelu, scale=sh2[:, o:o + 1]
                                   ).then_inc(F[n]["g3"], 1)

            def F1(b, with_f2):
                silus_F("f1", b)
                gelus2("f1", b, 0), gelus2("f1", b, 1), gelus3("f1", b, 0)
                if with_f2:
                    input_T("f2", b - 2)
                gelus3("f1", b, 1)

            def joined(b, n):
                src, dst, factor = join_result(n)
                act.wait_ge(j_full, b * NJ + n + 1)
                act.activation(dst, src, ACT.Copy, scale=factor).then_inc(j_act, 1)

            def N_T(b):
                act.wait_ge(n_tr, b + 1)
                act.activation(nT[:, :], bank[0][:, :], ACT.Identity, scale=ln1w, bias=ln1b).then_inc(n_nT, 1)

            def F2(b, with_join, with_n):
                silus_F("f2", b)
                for s in range(FFN_SLOTS):
                    if s == 3:
                        gelus2("f2", b, 0)
                    if s == 7:
                        gelus2("f2", b, 1)
                    if s == 11:
                        gelus3("f2", b, 0)
                    if s == 15:
                        gelus3("f2", b, 1)
                    n = s - (FFN_SLOTS - NJ)
                    if with_join and n >= 0 and n % 2 == 1:
                        joined(b + 1, n)
                    if s == 15 and with_n:
                        N_T(b + 2)

            def N_logs(b):
                act.wait_ge(n_abs, b * 2 + 2)
                act.activation(ez[:, :], absz[:, :], ACT.Exp, scale=-1.0).then_inc(n_exp, 1)
                act.wait_ge(n_exp, b + 1)
                act.activation(lz[:, :], ez[:, :], ACT.Ln, bias=1.0).then_inc(n_ln, 1)

            def decays(b, q):
                if q == 0:
                    act.wait_ge(n_bias, b + 1)
                act.wait_ge(d_sum, b * 8 + q + 1)
                for h in range(4):
                    u = 4 * q + h
                    last = act.activation(MT[:, u, :], heads(bank[2 + q % 2])[:, h, :], ACT.Exp, bias=biasj[:, u:u + 1])
                last.then_inc(d_exp, 1)

            def exps(b):
                act.wait_ge(n_gn, b + 1)
                if not isinstance(b, int) or b > 0:
                    act.wait_ge(s_S, b * 6)
                act.activation(eg[:, :], gn[:, 0:U], ACT.Exp)
                act.activation(egC[:, :], gn[:, U:2 * U], ACT.Exp).then_inc(p_gexp, 1)
                act.wait_ge(p_kdl, b + 1)
                act.activation(kds[:, :], kdl[:, :], ACT.Exp).then_inc(p_kds, 1)

            def silu(b, c, i):
                n = 6 * c + i
                bk = bank[6 + n % 2] if n < 4 else bank[n % 4]
                act.wait_ge(p_proj, b * 6 * NC + n + 1)
                dst = (qk[c % 2][:, i // 2, 4 * (i % 2):4 * (i % 2) + 4, :] if i < 4
                       else V[:, H * c + 4 * (i - 4):H * c + 4 * (i - 4) + 4, :])
                act.activation(dst, heads(bk), ACT.Silu).then_inc(p_silu, 1)

            def copy_T(b, c, i):
                n = 6 * c + i
                g = slice(4 * (i % 2), 4 * (i % 2) + 4)
                gu = slice(H * c + 4 * (i % 2), H * c + 4 * (i % 2) + 4)
                act.wait_ge(p_tr, b * 6 * NC + n + 1)
                act.activation((KT[:, gu, :], qT[:, g, :], QET[:, gu, :])[i // 2], heads(bank[4 + n % 2]), ACT.Copy
                               ).then_inc(p_trc, 1)

            def P(b, with_m, with_f1):
                silu(b, 0, 4), silu(b, 0, 5)
                for i in range(4):
                    silu(b, 1, i)
                for c in range(NC - 1):
                    copy_T(b, c, 0), copy_T(b, c, 1), silu(b, c + 1, 4), copy_T(b, c, 2), silu(b, c + 1, 5)
                    copy_T(b, c, 3), copy_T(b, c, 4)
                    if c == NC - 2 and with_m:
                        M_input(b - 1)
                    copy_T(b, c, 5)
                    if c < NC - 2:
                        for i in range(4):
                            silu(b, c + 2, i)
                if with_m:
                    M(b - 1)
                for i in range(6):
                    if i == 5 and with_f1:
                        input_T("f1", b + 1)
                    copy_T(b, NC - 1, i)

            def M_input(b):
                act.wait_ge(m_tr, b + 1)
                act.activation(xT[:, :], bank[0][:, :], ACT.Identity, scale=ln2w, bias=ln2b).then_inc(m_xT, 1)

            def M(b):
                for o in range(KB):
                    act.wait_ge(m_up, b * KB + o + 1)
                    act.activation(hid[0][:, o, :], bank[o][:, :], ACT.Gelu, bias=b1[:, o:o + 1]).then_inc(m_gelu, 1)

            def S(b, with_next):
                for c in range(NC):
                    for g in range(2):
                        u = slice(H * c + 4 * g, H * c + 4 * g + 4)
                        act.wait_ge(s_w, b * 8 + 2 * c + g + 1)
                        act.activation(V[:, u, :], heads(bank[4 + g]), ACT.Copy).then_inc(s_wc, 1)
                    if with_next and c == 0:
                        N_logs(b + 1)
                    if with_next and c > 0:
                        decays(b + 1, 2 * c - 2), decays(b + 1, 2 * c - 1)
                    for g in range(2):
                        if with_next and c == NC - 1:
                            silu(b + 1, 0, 2 * g), silu(b + 1, 0, 2 * g + 1)
                        act.wait_ge(s_o, b * 8 + 2 * c + g + 1)
                        act.activation(oT[:, 4 * g:4 * g + 4, :], heads(bank[g]), ACT.Copy).then_inc(s_oc, 1)
                if with_next:
                    decays(b + 1, 6), decays(b + 1, 7), exps(b + 1)

            act.wait_ge(ld_w, 3 * 16)
            input_T("f1", 0), F1(0, False), N_T(0), N_logs(0)
            for i in range(4):
                silu(0, 0, i)
            for q in range(8):
                decays(0, q)
            exps(0)
            P(0, False, True), F1(1, False)
            N_T(1)
            for n in range(1, NJ, 2):
                joined(0, n)
            S(0, True)
            with act.Fori(1, B - 1) as t:
                P(t, True, True), F1(t + 1, True), F2(t - 1, True, True), S(t, True)
            P(B - 1, True, False), input_T("f2", B - 2), F2(B - 2, False, False)
            for n in range(1, NJ, 2):
                joined(B - 1, n)
            S(B - 1, False)
            M_input(B - 1), M(B - 1), input_T("f2", B - 1), F2(B - 1, False, False)

        @block.tensor
        def _(pe):
            def transposes(rows, done):
                for c in range(NC):
                    last = pe.transpose(bank[0][:, 128 * c:128 * c + 128], rows[:, c, :], ident[:, :])
                last.then_inc(done, 1)

            def half_layer(w, src, k, pair, bk, done):
                for i in range(2):
                    o = 2 * pair + i
                    last = pe.matmul(bank[bk + i][:, :], w[:, k, 128 * o:128 * o + 128], src[:, k, :],
                                     start=(k == 0), stop=(k == KB - 1))
                    if k == KB - 1:
                        last.then_inc(done, 1)

            def down(w, src, k, done):
                for c in range(NC):
                    last = pe.matmul(bank[4][:, 128 * c:128 * c + 128], src[:, k, 128 * c:128 * c + 128], w[:, k, :],
                                     start=(k == 0 and c == 0), stop=(k == KB - 1), skip_group_check=True)
                if k == KB - 1:
                    last.then_inc(done, 1)

            def input_T(n, b):
                pe.wait_ge(ln_f[n].rows, b + 1)
                transposes(xn if n == "f2" else xin, F[n]["tr"])

            def layer1(n, b, blocks):
                f = F[n]
                for o in blocks:
                    if o == 0:
                        pe.wait_ge(f["xT"], b + 1)
                    if o >= 2:
                        pe.wait_ge(f["hid"], b * KB + o - 1)
                    for w, bk in ((w1, 2 * (o % 2)), (w2, 2 * (o % 2) + 1)):
                        pe.matmul(bank[bk][:, :], w[:, 128 * o:128 * o + 128], xT[:, :], start=True, stop=True
                                  ).then_inc(f["gate"], 1)

            def slot(n, b, s):
                f, part, k = F[n], s // KB, s % KB
                if part == 0:
                    pe.wait_ge(f["hid"], b * KB + k + 1)
                    half_layer(h1, own[n], k, 0, 4, f["l2"])
                elif part == 1:
                    half_layer(h1, own[n], k, 1, 0, f["l2"])
                elif part == 2:
                    pe.wait_ge(f["g2"], b * KB + (2 if k == 0 else k + 1))
                    half_layer(h2, other[n], k, 0, 4, f["l3"])
                elif part == 3:
                    half_layer(h2, other[n], k, 1, 2, f["l3"])
                else:
                    pe.wait_ge(f["g3"], b * KB + k + 1)
                    down(w3, own[n], k, f["l4"])

            def F1(b, with_m, with_f2):
                if with_m:
                    pe.wait_ge(m_gelu, (b - 2) * KB + KB)
                layer1("f1", b, (0, 1))
                if isinstance(b, int) and b == 0:
                    pe.wait_ge(ld_h, 5 * 16)
                if not isinstance(b, int) or b > 0:
                    pe.wait_ge(p_trc, b * 6 * NC)
                if with_m:
                    M_down(b - 2)
                layer1("f1", b, (2, 3))
                if with_m:
                    pe.wait_ge(m_x2, b - 1)
                for s in range(FFN_SLOTS):
                    if s == 3 * KB and with_f2:
                        input_T("f2", b - 2)
                    if s == 4 * KB and with_f2:
                        layer1("f2", b - 2, (0,))
                        pe.wait_ge(F["f1"]["g3"], b * KB + KB)
                        layer1("f2", b - 2, (1,))
                    slot("f1", b, s)

            def F2(b, started, with_join, with_n):
                layer1("f2", b, (2, 3) if started else ALL)
                for s in range(FFN_SLOTS):
                    if s == 0 and started:
                        pe.wait_ge(F["f1"]["sc"], b + 3)
                    n = s - (FFN_SLOTS - NJ)
                    if with_join and n >= 0:
                        join_waits(b + 1, n)
                    slot("f2", b, s)
                    if with_join and n >= 0:
                        join(b + 1, n)
                    if s == 4 * KB - 1 and with_n:
                        N_T(b + 2)

            def N_T(b):
                pe.wait_ge(ln_n1.rows, b + 1)
                transposes(xn1, n_tr)

            def N_logits(b):
                pe.wait_ge(n_nT, b + 1)
                for c in range(NC):
                    last = pe.matmul(bank[2][:, 16 * c:16 * c + 16], nT[:, 128 * c:128 * c + 128], wba[:, :],
                                     start=True, stop=True)
                last.then_inc(n_logit, 1)

            def N_sums(b):
                pe.wait_ge(n_lo, b + 1)
                pe.matmul(bank[2][:, 2 * U:3 * U], triu[:, :], lga[:, :], start=True, stop=True)
                pe.matmul(bank[2][:, 3 * U:4 * U], ones[:, :].to_broadcast([128, 128]), lga[:, :], start=True, stop=True
                          ).then_inc(n_g, 1)

            def decay(b, q):
                if q >= 2:
                    pe.wait_ge(d_exp, b * 8 + q - 1)
                bk = bank[2 + q % 2]
                pe.matmul(bk[:, :], identb[:, :], maskb[:, :].unsqueeze(1).to_broadcast([128, 4, 128]),
                          start=True, stop=False, skip_group_check=True)
                for h in range(4):
                    u = 4 * q + h
                    for part in (lah, lal):
                        last = pe.matmul(heads(bk)[:, h, :], part[:, u:u + 1].to_broadcast([128, 128]), triur[:, :],
                                         start=False, stop=(part is lal and h == 3), skip_group_check=True)
                last.then_inc(d_sum, 1)

            def proj(b, c, i):
                n = 6 * c + i
                if 2 <= n < 4:
                    pe.wait_ge(p_silu, b * 6 * NC + n - 1)
                if n >= 8:
                    pe.wait_ge(p_silu, b * 6 * NC + n - 3)
                bk = bank[6 + n % 2] if n < 4 else bank[n % 4]
                pe.matmul(bk[:, :], nT[:, 128 * c:128 * c + 128], wqkv[:, i // 2, 512 * (i % 2):512 * (i % 2) + 512],
                          start=True, stop=True).then_inc(p_proj, 1)

            def turn(b, c, i):
                n = 6 * c + i
                if i == 0:
                    pe.wait_ge(p_unit, b * NC + c + 1)
                if i == 4:
                    pe.wait_ge(p_qe, b * NC + c + 1)
                if n >= 2:
                    pe.wait_ge(p_trc, b * 6 * NC + n - 1)
                for h in range(4):
                    hh = 4 * (i % 2) + h
                    src = (qk[c % 2][:, 1, hh, :], qk[c % 2][:, 0, hh, :], qe[:, hh, :])[i // 2]
                    last = pe.transpose(bank[4 + n % 2][:, 128 * h:128 * h + 128], src, ident[:, :])
                last.then_inc(p_tr, 1)

            def products(b, c, g, s):
                k = 4 * c + 2 * g + s
                if k < 2:
                    pe.wait_ge(p_silu, b * 6 * NC + 4)
                else:
                    pe.wait_ge(p_am, b * 16 + k - 1)
                pe.wait_ge(p_trc, b * 6 * NC + 6 * c + 1 + g + 2 * s)
                for h in range(4):
                    u = H * c + 4 * g + h
                    last = pe.matmul(heads(bank[6 + s])[:, h, :], KT[:, u, :], (KT[:, u, :], qT[:, 4 * g + h, :])[s],
                                     start=True, stop=True)
                last.then_inc(p_kq, 1)

            def P(b, with_m, with_f1):
                if isinstance(b, int) and b == 0:
                    pe.wait_ge(F["f1"]["sc"], 1)
                else:
                    pe.wait_ge(s_oc, b * 8)
                    pe.wait_ge(s_xa, b * NC)
                proj(b, 0, 4), proj(b, 0, 5)
                pe.wait_ge(d_exp, b * 8 + 8)
                for i in range(4):
                    proj(b, 1, i)
                for c in range(NC):
                    if c == NC - 1 and with_m:
                        M_up(b - 1)
                    turn(b, c, 0), turn(b, c, 1)
                    if c < NC - 1:
                        proj(b, c + 1, 4)
                    turn(b, c, 2)
                    if c < NC - 1:
                        proj(b, c + 1, 5)
                    turn(b, c, 3)
                    products(b, c, 0, 0), turn(b, c, 4), products(b, c, 0, 1)
                    if c == NC - 2 and with_m:
                        pe.wait_ge(p_silu, b * 6 * NC + 6 * NC - 3)
                        M_T(b - 1)
                    if c == NC - 1 and with_f1:
                        if with_m:
                            pe.wait_ge(m_gelu, (b - 1) * KB + 1)
                        else:
                            pe.wait_ge(p_silu, b * 6 * NC + 6 * NC)
                        input_T("f1", b + 1)
                    turn(b, c, 5), products(b, c, 1, 0), products(b, c, 1, 1)
                    if c < NC - 2:
                        for i in range(4):
                            proj(b, c + 2, i)

            def M_T(b):
                pe.wait_ge(ln_m.rows, b + 1)
                transposes(xa, m_tr)

            def M_up(b):
                pe.wait_ge(m_xT, b + 1)
                if not (isinstance(b, int) and b == B - 1):
                    pe.wait_ge(p_silu, b * 6 * NC + 12 * NC)
                for o in range(KB):
                    pe.matmul(bank[o][:, :], wm1[:, 128 * o:128 * o + 128], xT[:, :], start=True, stop=True
                              ).then_inc(m_up, 1)

            def M_down(b):
                for k in range(KB):
                    pe.wait_ge(m_gelu, b * KB + k + 1)
                    down(wm2, hid[0], k, m_down)

            def hold(bk):
                pe.matmul(bk[:, 0:1], ident[:, :], ident[:, 0:1], start=True, stop=True)

            def join_waits(b, n):
                if n == 0:
                    pe.wait_ge(b_TB, b * 3 * 16 + 3 * 16)
                if n == 4:
                    pe.wait_ge(b_Rin, b * 4 * 16 + 4 * 16)
                if n >= 2:
                    pe.wait_ge((j_dve, j_act)[n % 2], b * (NJ // 2) + n // 2)

            def join(b, n):
                kind, part = JOINS[n]
                bk = bank[6 + n % 2]
                if kind in ("p64", "r64"):
                    for i in range(8):
                        u = 8 * part + i
                        col = slice(64 * i, 64 * i + 64)
                        if kind == "p64":
                            last = pe.matmul(bk[64:128, col], R[0:64, u, 64:128], TB[0:64, u, :], start=True, stop=True)
                        else:
                            last = pe.matmul(bk[0:64, col], TB[64:128, u, :], R[64:128, u, 64:128], start=True, stop=True)
                else:
                    pair, half = part
                    e, o = slice(64 * pair, 64 * pair + 32), slice(64 * pair + 32, 64 * pair + 64)
                    for i in range(16):
                        u = 16 * half + i
                        col = slice(32 * i, 32 * i + 32)
                        if kind == "p32":
                            last = pe.matmul(bk[o, col], R[e, u, o], TB[e, u, 0:32], start=True, stop=True)
                        elif kind == "r32":
                            last = pe.matmul(bk[e, col], TB[o, u, 0:32], R[o, u, o], start=True, stop=True)
                        else:
                            last = pe.matmul(bk[o, col], R[o, u, o], TB[o, u, 0:32], start=True, stop=True)
                last.then_inc(j_full, 1)

            def J(b):
                for n in range(NJ):
                    join_waits(b, n)
                    hold(bank[6 + n % 2])
                    join(b, n)

            def S(b, with_next):
                if isinstance(b, int) and b == 0:
                    pe.wait_ge(F["f1"]["sc"], 2)
                else:
                    pe.wait_ge(F["f2"]["sc"], b)
                pe.wait_ge(j_dve, b * (NJ // 2) + NJ // 2)
                pe.wait_ge(j_act, b * (NJ // 2) + NJ // 2)
                for c in range(NC):
                    if c > 0:
                        if with_next and c == 1:
                            pe.wait_ge(n_bias, b + 2)
                        if with_next and c > 1:
                            pe.wait_ge(d_exp, (b + 1) * 8 + 2 * c - 2)
                        for g in range(2):
                            pe.wait_ge(s_S, b * 6 + 2 * (c - 1) + g + 1)
                            for h in range(4):
                                u = H * c + 4 * g + h
                                last = pe.matmul(heads(bank[2 + g])[:, h, :], KT[:, u, :], state[:, 4 * g + h, :],
                                                 start=True, stop=True)
                            last.then_inc(s_ks, 1)
                    for g in range(2):
                        if c > 0:
                            for h in range(4):
                                pe.matmul(heads(bank[g])[:, h, :], state[:, 4 * g + h, :], QET[:, H * c + 4 * g + h, :],
                                          start=(h == 0), stop=False, skip_group_check=True)
                            pe.wait_ge(s_rhs, b * 6 + 2 * (c - 1) + g + 1)
                            if g == 0:
                                pe.wait_ge(s_xa, b * NC + c)
                        for h in range(4):
                            u = H * c + 4 * g + h
                            last = pe.matmul(heads(bank[4 + g])[:, h, :], R[:, u, :], V[:, u, :], start=True, stop=True)
                        last.then_inc(s_w, 1)
                    if with_next and c > 0:
                        decay(b + 1, 2 * c - 2), decay(b + 1, 2 * c - 1)
                    for g in range(2):
                        if c < NC - 1:
                            pe.wait_ge(s_wc, b * 8 + 2 * c + g + 1)
                            for h in range(4):
                                u = H * c + 4 * g + h
                                last = pe.matmul(heads(bank[6 + g])[:, h, :], KD[:, u, :], V[:, u, :], start=True, stop=True)
                            last.then_inc(s_up, 1)
                        elif with_next:
                            proj(b + 1, 0, 2 * g), proj(b + 1, 0, 2 * g + 1)
                        pe.wait_ge(s_wc, b * 8 + 2 * c + g + 1)
                        for h in range(4):
                            u = H * c + 4 * g + h
                            last = pe.matmul(heads(bank[g])[:, h, :], V[:, u, :], MT[:, u, :],
                                             start=(c == 0 and h == 0), stop=True, skip_group_check=True)
                        last.then_inc(s_o, 1)
                    for g in range(2):
                        if with_next and c == 0 and g == 1:
                            N_sums(b + 1)
                        pe.wait_ge(s_oc, b * 8 + 2 * c + g + 1)
                        for h in range(4):
                            hh = 4 * g + h
                            last = pe.matmul(bank[4][:, 0:D], oT[:, hh, :], wo[:, hh, :], start=(hh == 0), stop=(hh == H - 1))
                    last.then_inc(s_y, 1)
                if with_next:
                    decay(b + 1, 6), decay(b + 1, 7)

            pe.wait_ge(c_pool, 1)
            input_T("f1", 0)
            pe.wait_ge(ld_w, 3 * 16)
            F1(0, False, False)
            pe.wait_ge(ld_a, 8 * 16)
            pe.wait_ge(c_dve, 1)
            N_T(0), N_logits(0)
            for i in range(4):
                proj(0, 0, i)
            N_sums(0)
            pe.wait_ge(n_bias, 1)
            for q in range(8):
                decay(0, q)
            P(0, False, True), F1(1, False, False)
            N_T(1), N_logits(1), J(0), S(0, True)
            with pe.Fori(1, B - 1) as t:
                P(t, True, True), F1(t + 1, True, True), F2(t - 1, True, True, True), N_logits(t + 1), S(t, True)
            P(B - 1, True, False)
            pe.wait_ge(p_trc, B * 6 * NC)
            M_down(B - 2)
            input_T("f2", B - 2), F2(B - 2, False, False, False), J(B - 1), S(B - 1, False)
            pe.wait_ge(s_oc, B * 8)
            M_T(B - 1), M_up(B - 1)
            pe.wait_ge(s_xa, B * NC)
            M_down(B - 1)
            input_T("f2", B - 1), F2(B - 1, False, False, False)


def kernel(**inputs):
    import numpy as np
    import concourse.bacc as bacc
    from concourse.bass_utils import run_bass_kernel_spmd

    a = {k: np.asarray(v) for k, v in inputs.items()}
    at, ff = "L0_attn_", "L0_ffn_"

    def column_blocks(v):
        return v.reshape(KB, 128).T

    cols = [column_blocks(a[ff + k]) for k in ("w1_s", "w2_s", "h1_s", "h2_s")] + [column_blocks(a[at + "b1"])]
    cols += [a[at + k].reshape(128, 1) for k in ("ln1_w", "ln1_b", "ln2_w", "ln2_b")]
    host = {
        "x": a[at + "x"], "w1T": a[ff + "w1_w"].T, "w2T": a[ff + "w2_w"].T, "h1T": a[ff + "h1_w"].T,
        "h2T": a[ff + "h2_w"].T, "w3T": a[ff + "w3_w"].T, "s3": a[ff + "w3_s"], "b2": a[at + "b2"],
        "cols": np.concatenate(cols, axis=1),
    }
    host.update({k: a[at + k] for k in ("Wq", "Wk", "Wv", "Wb", "Wa", "Wo", "W1", "W2")})

    nc = bacc.Bacc("TRN2", target_bir_lowering=False, num_devices=1)
    arrays, aps = {}, {}
    for name, v in host.items():
        arrays["in_" + name] = np.ascontiguousarray(v)
        aps[name] = nc.dram_tensor("in_" + name, v.shape, mybir.dt.from_np(v.dtype), kind="ExternalInput").ap()
    aps["out"] = nc.dram_tensor("out_x", (B, T, D), mybir.dt.float32, kind="ExternalOutput").ap()
    build_program(nc, aps)
    r = run_bass_kernel_spmd(nc, [arrays], core_ids=[0])
    return r.results[0]["out_x"]
```
